# Optimizing a Trainium2 kernel written in Bass

```python
import numpy as np
import jax
import jax.numpy as jnp

def _softmax(x, axis=-1):
    return jax.nn.softmax(x, axis=axis)

def _gelu(x):
    return jax.nn.gelu(x, approximate=True)

def _silu(x):
    return jax.nn.silu(x)

def _sigmoid(x):
    return jax.nn.sigmoid(x)

def _layernorm(x, axis=-1, eps=1e-05):
    m = jnp.mean(x, axis=axis, keepdims=True)
    v = jnp.var(x, axis=axis, keepdims=True)
    return (x - m) / jnp.sqrt(v + eps)

def _scatter_add(tgt, idx, src, axis=0):
    return tgt.at[idx].add(src)

def _segment_sum(src, seg, n):
    return jax.ops.segment_sum(src, seg, n)
kernel_name = 'mk_adj_resnorm_d2_adj_r2_62ec80'

def setup_inputs(seed: int=0):
    np.random.seed(seed)
    _w = jnp.asarray

    def _rec_inputs():
        import jax
        import jax.numpy as jnp
        _gk = jax.random.key(seed)
        x = -0.0005207 + 1.001 * jax.random.normal(jax.random.fold_in(_gk, 1), (4096, 128), jnp.float32)
        _a = jax.random.bernoulli(jax.random.fold_in(_gk, 2), 0.000976562, (4096, 4096))
        _a = jnp.logical_or(_a, jnp.eye(4096, dtype=bool))
        _af = _a.astype(jnp.float32)
        _af = _af * jax.random.uniform(jax.random.fold_in(_gk, 3), (4096, 4096), jnp.float32, 0.05, 1)
        adj = _af
        return (x, adj)
    x, adj = _rec_inputs()

    def _L0_gnn_setup():
        import jax, jax.numpy as jnp
        import numpy as np
        THRESH = 1e-06
        EPS = 1e-08
        LN_EPS = 1e-05

        def _layer(h, M, W_in, b_in, W_out, b_out, W_self, b_self, gamma, beta):
            A = M / (jnp.sum(M, axis=0, keepdims=True) + EPS)
            mask = A > THRESH
            W = jnp.where(mask, A, 0.0)
            T = h @ W_in + b_in
            weighted_sum = jnp.einsum('ji,jd->id', W, T)
            weight_sum = jnp.sum(W, axis=0)
            has_edge = jnp.any(mask, axis=0)
            agg = jnp.where(has_edge[:, None], weighted_sum / (weight_sum[:, None] + EPS), T)
            agg = agg @ W_out + b_out
            out = agg + (h @ W_self + b_self)
            mu = jnp.mean(out, axis=-1, keepdims=True)
            var = jnp.mean(jnp.square(out - mu), axis=-1, keepdims=True)
            out = (out - mu) * jax.lax.rsqrt(var + LN_EPS) * gamma + beta
            return out
        key = jax.random.key(seed)
        ks = jax.random.split(key, 16)
        N, D_IN, D_H, D_OUT = (4096, 128, 256, 128)
        s = 0.05
        return {'node_features': jax.random.normal(ks[0], (N, D_IN), jnp.float32), 'mobility_matrix': jax.random.uniform(ks[1], (N, N), jnp.float32), 'W_in1': jax.random.normal(ks[2], (D_IN, D_H)) * s, 'b_in1': jnp.zeros((D_H,)), 'W_out1': jax.random.normal(ks[3], (D_H, D_H)) * s, 'b_out1': jnp.zeros((D_H,)), 'W_self1': jax.random.normal(ks[4], (D_IN, D_H)) * s, 'b_self1': jnp.zeros((D_H,)), 'g1': jnp.ones((D_H,)), 'be1': jnp.zeros((D_H,)), 'W_in2': jax.random.normal(ks[5], (D_H, D_OUT)) * s, 'b_in2': jnp.zeros((D_OUT,)), 'W_out2': jax.random.normal(ks[6], (D_OUT, D_OUT)) * s, 'b_out2': jnp.zeros((D_OUT,)), 'W_self2': jax.random.normal(ks[7], (D_H, D_OUT)) * s, 'b_self2': jnp.zeros((D_OUT,)), 'g2': jnp.ones((D_OUT,)), 'be2': jnp.zeros((D_OUT,))}
    _L0_gnn_all = _L0_gnn_setup()
    _L0_gnn_in = {k: v for k, v in _L0_gnn_all.items() if k in ('W_in1', 'b_in1', 'W_out1', 'b_out1', 'W_self1', 'b_self1', 'g1', 'be1', 'W_in2', 'b_in2', 'W_out2', 'b_out2', 'W_self2', 'b_self2', 'g2', 'be2')}
    del _L0_gnn_all

    def _L1_gnn_setup():
        import jax, jax.numpy as jnp
        import numpy as np
        N = 4096
        D_IN = 128
        D_OUT = 128
        key = jax.random.key(seed)
        k_x, k_a, k_w, k_bias = jax.random.split(key, 4)
        x = jax.random.normal(k_x, (N, D_IN), dtype=jnp.float32)
        A_shape = jax.random.randint(k_a, (N, N), 0, 2).astype(jnp.float32)
        A_shape = A_shape.at[jnp.arange(N), jnp.arange(N)].set(1.0)
        lim = 1.0 / np.sqrt(D_IN)
        W = jax.random.uniform(k_w, (D_OUT, D_IN), jnp.float32, -lim, lim)
        bias = jax.random.uniform(k_bias, (D_OUT,), jnp.float32, -lim, lim)
        b = jnp.ones((1,), dtype=jnp.float32)
        return {'x': x, 'A_shape': A_shape, 'W': W, 'bias': bias, 'b': b}
    _L1_gnn_all = _L1_gnn_setup()
    _L1_gnn_in = {k: v for k, v in _L1_gnn_all.items() if k in ('W', 'bias', 'b')}
    del _L1_gnn_all
    return {'x': x, 'adj': adj, 'L0_gnn_W_in1': _L0_gnn_in['W_in1'], 'L0_gnn_b_in1': _L0_gnn_in['b_in1'], 'L0_gnn_W_out1': _L0_gnn_in['W_out1'], 'L0_gnn_b_out1': _L0_gnn_in['b_out1'], 'L0_gnn_W_self1': _L0_gnn_in['W_self1'], 'L0_gnn_b_self1': _L0_gnn_in['b_self1'], 'L0_gnn_g1': _L0_gnn_in['g1'], 'L0_gnn_be1': _L0_gnn_in['be1'], 'L0_gnn_W_in2': _L0_gnn_in['W_in2'], 'L0_gnn_b_in2': _L0_gnn_in['b_in2'], 'L0_gnn_W_out2': _L0_gnn_in['W_out2'], 'L0_gnn_b_out2': _L0_gnn_in['b_out2'], 'L0_gnn_W_self2': _L0_gnn_in['W_self2'], 'L0_gnn_b_self2': _L0_gnn_in['b_self2'], 'L0_gnn_g2': _L0_gnn_in['g2'], 'L0_gnn_be2': _L0_gnn_in['be2'], 'L1_gnn_W': _L1_gnn_in['W'], 'L1_gnn_bias': _L1_gnn_in['bias'], 'L1_gnn_b': _L1_gnn_in['b']}

def reference(x, adj, L0_gnn_W_in1, L0_gnn_b_in1, L0_gnn_W_out1, L0_gnn_b_out1, L0_gnn_W_self1, L0_gnn_b_self1, L0_gnn_g1, L0_gnn_be1, L0_gnn_W_in2, L0_gnn_b_in2, L0_gnn_W_out2, L0_gnn_b_out2, L0_gnn_W_self2, L0_gnn_b_self2, L0_gnn_g2, L0_gnn_be2, L1_gnn_W, L1_gnn_bias, L1_gnn_b):
    import jax
    import jax.numpy as jnp

    def _L0_gnn_ref(node_features, mobility_matrix, W_in1, b_in1, W_out1, b_out1, W_self1, b_self1, g1, be1, W_in2, b_in2, W_out2, b_out2, W_self2, b_self2, g2, be2):
        import jax, jax.numpy as jnp
        import numpy as np
        THRESH = 1e-06
        EPS = 1e-08
        LN_EPS = 1e-05

        def _layer(h, M, W_in, b_in, W_out, b_out, W_self, b_self, gamma, beta):
            A = M / (jnp.sum(M, axis=0, keepdims=True) + EPS)
            mask = A > THRESH
            W = jnp.where(mask, A, 0.0)
            T = h @ W_in + b_in
            weighted_sum = jnp.einsum('ji,jd->id', W, T)
            weight_sum = jnp.sum(W, axis=0)
            has_edge = jnp.any(mask, axis=0)
            agg = jnp.where(has_edge[:, None], weighted_sum / (weight_sum[:, None] + EPS), T)
            agg = agg @ W_out + b_out
            out = agg + (h @ W_self + b_self)
            mu = jnp.mean(out, axis=-1, keepdims=True)
            var = jnp.mean(jnp.square(out - mu), axis=-1, keepdims=True)
            out = (out - mu) * jax.lax.rsqrt(var + LN_EPS) * gamma + beta
            return out
        h = _layer(node_features, mobility_matrix, W_in1, b_in1, W_out1, b_out1, W_self1, b_self1, g1, be1)
        h = jax.nn.relu(h)
        h = _layer(h, mobility_matrix, W_in2, b_in2, W_out2, b_out2, W_self2, b_self2, g2, be2)
        h = jax.nn.relu(h)
        return h

    def _L1_gnn_ref(x, A_shape, W, bias, b):
        import jax, jax.numpy as jnp
        import numpy as np
        N = 4096
        D_IN = 128
        D_OUT = 128
        y = jnp.linalg.norm(x, axis=-1, keepdims=True)
        A = x @ x.T / (y @ y.T)
        A = A * b
        A = jnp.tanh(A / 8.0) * 8.0
        A = jnp.exp(A) * A_shape
        A = A / jnp.sum(A, axis=-1, keepdims=True)
        x = A @ x
        return x @ W.T + bias
    x = _layernorm(x + _L0_gnn_ref(x, adj, L0_gnn_W_in1, L0_gnn_b_in1, L0_gnn_W_out1, L0_gnn_b_out1, L0_gnn_W_self1, L0_gnn_b_self1, L0_gnn_g1, L0_gnn_be1, L0_gnn_W_in2, L0_gnn_b_in2, L0_gnn_W_out2, L0_gnn_b_out2, L0_gnn_W_self2, L0_gnn_b_self2, L0_gnn_g2, L0_gnn_be2), axis=-1)
    x = _layernorm(x + _L1_gnn_ref(x, adj, L1_gnn_W, L1_gnn_bias, L1_gnn_b), axis=-1)
    return x

_drawn_inputs = setup_inputs


def setup_inputs(seed=0):
    import zlib

    import numpy as np

    out = dict(_drawn_inputs(seed))
    spreads = {'L0_gnn_b_in1': (0.0, 0.1),
     'L0_gnn_b_out1': (0.0, 0.1),
     'L0_gnn_b_self1': (0.0, 0.1),
     'L0_gnn_g1': (1.0, 0.2),
     'L0_gnn_be1': (0.0, 0.1),
     'L0_gnn_b_in2': (0.0, 0.1),
     'L0_gnn_b_out2': (0.0, 0.1),
     'L0_gnn_b_self2': (0.0, 0.1),
     'L0_gnn_g2': (1.0, 0.2),
     'L0_gnn_be2': (0.0, 0.1)}
    factors = {}
    for name, (base, spread) in spreads.items():
        noise = np.random.default_rng([zlib.crc32(name.encode()), seed]).standard_normal(out[name].shape)
        drawn = base * np.exp(spread * noise) if base else spread * noise
        out[name] = jnp.asarray(drawn.astype(out[name].dtype))
    for name, factor in factors.items():
        out[name] = (out[name] * factor).astype(out[name].dtype)
    return out
```

```python
from contextlib import ExitStack

import concourse.bass as bass
from concourse import mybir

F32 = mybir.dt.float32
F32R = mybir.dt.float32r
I8 = mybir.dt.int8
I32 = mybir.dt.int32
ALU = mybir.AluOpType
ACT = mybir.ActivationFunctionType
AX = mybir.AxisListType

THRESH = 1e-6
EPS = 1e-8
LN_EPS = 1e-5
TANH_RANGE = 8.0

W = 512
B = W // 128
GROUPS = 4
SBUF_START = 16512
SBUF_END = 229344
KIB = 1024


class Links:

    def __init__(self, eng, sem, count, panel, before=0):
        self.eng, self.sem, self.first, self.n = eng, sem, panel * count, before

    def __call__(self, ins):
        ins.then_inc(self.sem, 1)
        self.n += 1
        self.eng.wait_ge(self.sem, self.first + self.n)


def build_program(nc, t):
    NB = t["x"].shape[1]
    TILES = NB
    N = NB * 128
    P = N // W
    TG = TILES // GROUPS
    PAIRS = TILES // 2
    LOOPS = (P - 2) // 2
    D, H = 128, 256
    HALF = TG * W // 2

    ctx = ExitStack()
    with ctx:
        place = [SBUF_START]

        def at(name, shape, dt=F32, offset=None):
            size = 1 if dt == I8 else 4
            for s in shape[1:]:
                size *= s
            if offset is None:
                offset = place[0]
                place[0] += (size + 31) // 32 * 32
            return nc.alloc_sbuf_tensor_at(name, shape, dt, offset=offset)

        def sem(name):
            return ctx.enter_context(nc.semaphore(name))

        adjA = at("adjA", [128, TILES, W])
        b_start = place[0]
        adjB = at("adjB", [128, TILES, W])
        b_end = place[0] = b_start + 64 * KIB
        adj_of = (adjA, adjB)
        x = at("x_nodes", [128, NB, D])
        tc_start = place[0]
        tc = at("t2_self2", [128, NB, 2 * D])
        xT = at("xT_panel", [128, W])
        w_self1 = at("w_self1_sb", [128, H])
        w_cat2 = at("w_in2_self2", [128, 2, 2 * D])
        v1 = at("w_in1_w_out1", [128, H])
        brow1 = at("bias_rows1", [35, H])
        lrow1 = at("bias_left1", [35, W])
        bias2 = at("bias2", [128, 2 * D])
        ident = at("ident", [128, 128])
        ones = at("ones", [128, 128])
        layer1_start = place[0]
        sums = at("column_sums", [128, 2, W])
        part = at("part_sums", [128, W])
        thr = at("thresholds", [128, W])
        ysum = at("edge_sums", [128, W])
        q = at("q_row", [128, W])
        xs = at("scaled_x", [128, W])
        zn = at("z_normed", [128, 2, H])
        h1T = at("h1T", [128, 2, 2, 128])
        junk = at("sign_out", [128, 2048], I8)
        layer1_end = place[0]
        g1c = at("gamma1", [128, 2])
        be1c = at("beta1", [128, 2])
        q_col = at("q_col", [128, NB])
        no_edge = at("no_edge", [128, NB])
        minus_half = at("minus_half", [128, B])
        eps_row = at("eps_row", [128, B])
        width_row = at("width_row", [128, B])
        counts = at("sign_counts", [128, 2, 2 * GROUPS])
        cdiff = at("count_diff", [128, 1])
        cmax = at("sum_max", [128, 1])
        ntheta = at("minus_theta", [128, 1])
        flag = at("flag", [1, 1], I32)
        bns = at("bn_stats_out", [128, B, 6])
        mv = at("mean_var", [128, B, 2])
        vtmp = at("var_tmp", [128, B])
        rstd = at("rstd", [128, B])
        b_eighth = at("b_eighth", [128, 1])
        idle = at("idle", [1, 1])
        assert place[0] <= SBUF_END, place[0]
        w_in1T = at("w_in1T_sb", [128, 2, D], offset=tc_start)
        w_out1 = at("w_out1_sb", [128, 2, H], offset=tc_start + KIB)
        b_in1 = at("b_in1_sb", [128, 2], offset=tc_start + 3 * KIB)
        b_self2 = at("b_self2_sb", [128, D], offset=tc_start + 4 * KIB)
        place[0] = b_start
        uTh = at("uT_high", [128, N], F32R)
        uTl = at("uT_low", [128, N], F32R)
        w_out2 = at("w_out2_sb", [128, D])
        w3T = at("w3T_sb", [128, D])
        gamma2 = at("gamma2", [128, D])
        beta2 = at("beta2", [128, D])
        bias3 = at("bias3_sb", [128, D])
        loop_d = at("self_loops", [128, B, 128])
        t2s = at("t2_blocks", [128, B, D])
        xs2 = at("x_out", [128, W])
        r = at("rows", [128, B, D])
        r2 = at("rows_out", [128, B, D])
        mv2 = at("mean_var2", [128, B, 2])
        vtmp2 = at("var_tmp2", [128, 2, B])
        rstd2 = at("rstd2", [128, 2, B])
        rden = at("inv_weight_sum", [128, B])
        pr = at("weights3", [128, 4, 2 * W])
        assert place[0] <= b_end, (place[0], b_end)
        place[0] = layer1_start
        e = at("exp_out", [128, 2, 2 * W])
        den = at("weight_sums", [128, 2, 2 * W])
        assert place[0] <= layer1_end, (place[0], layer1_end)

        xp = ctx.enter_context(nc.psum_tensor("xp", [128, 2, W], F32))
        st = ctx.enter_context(nc.psum_tensor("st", [128, W], F32))
        sm = ctx.enter_context(nc.psum_tensor("sm", [128, W], F32))
        big = ctx.enter_context(nc.psum_tensor("big", [128, 4, W], F32))
        st4 = st[:, :].rearrange("p (b d) -> p b d", b=B)

        def z_of(b):
            return big[:, b // 2, (b % 2) * H:(b % 2 + 1) * H]

        slot_in = [[sem(f"slot_in{i}{g}") for g in range(GROUPS)] for i in range(2)]
        x_in = sem("x_in")
        xT_in = sem("xT_in")
        consts_in = sem("consts_in")
        consts2_in = sem("consts2_in")
        brow_copied = sem("brow_copied")
        ident_zero = sem("ident_zero")
        pool_consts = sem("pool_consts")
        dve_consts = sem("dve_consts")
        setup_mm = sem("setup_mm")
        weights_ready = sem("weights_ready")
        sums_links = sem("sums_links")
        csum_done = sem("csum_done")
        theta_links = sem("theta_links")
        theta_ready = sem("theta_ready")
        thr_ready = sem("thr_ready")
        signs_done = sem("signs_done")
        flag_links = sem("flag_links")
        diff_ready = sem("diff_ready")
        count_done = sem("count_done")
        panel_ready = sem("panel_ready")
        ysum_done = sem("ysum_done")
        stats_links = sem("stats_links")
        stats_ready = sem("stats_ready")
        cols_done = sem("cols_done")
        cols_read = sem("cols_read")
        main1 = sem("main1_group")
        evac1_links = sem("evac1_links")
        evac1 = sem("evac1_done")
        z_done = sem("z_done")
        ln1_links = sem("ln1_links")
        ln1_stats = sem("ln1_stats")
        pool1_links = sem("pool1_links")
        rstd1 = sem("rstd1_ready")
        zn_ready = sem("zn_ready")
        hT_done = sem("hT_done")
        h1T_ready = sem("h1T_ready")
        tc_psum = sem("tc_psum_done")
        tc_ready = sem("tc_ready")
        main2 = sem("main2_group")
        loops_ready = sem("loops_ready")
        t2s_ready = sem("t2s_ready")
        evac2 = sem("evac2_done")
        z2_done = sem("z2_done")
        ln2_links = sem("ln2_links")
        ln2_stats = sem("ln2_stats")
        pool2_links = sem("pool2_links")
        rstd2_ready = sem("rstd2_ready")
        u_ready = sem("u_ready")
        uT_done = sem("uT_psum_done")
        uTh_ready = sem("uTh_ready")
        uTl_ready = sem("uTl_ready")
        s_done = sem("s_done")
        tanh_done = sem("tanh_done")
        exp_done = sem("exp_done")
        w_ready = sem("w_ready")
        den_added = sem("den_added")
        pv_done = sem("pv_done")
        evac3 = sem("evac3_done")
        z3_done = sem("z3_done")
        ln3_links = sem("ln3_links")
        ln3_stats = sem("ln3_stats")
        pool3_links = sem("pool3_links")
        rstd3 = sem("rstd3_ready")
        out_ready = sem("out_ready")
        out_stored = sem("out_stored")

        MATRICES = ((w_in1T, "w_in1T"), (w_out1, "w_out1"), (w_cat2, "w_cat2"))
        ROWS = ((b_in1, "b_in1"), (w_self1, "w_self1"), (g1c, "g1"), (be1c, "be1"), (b_self2, "b_self2"),
                (b_eighth, "b"))
        N_CONSTS = len(MATRICES) + len(ROWS) + 4

        def panels(eng, step):
            with eng.Fori(0, LOOPS) as i:
                step(i * 2 + 1, 1)
                step(i * 2 + 2, 0)

        def layer1_panels(eng, step):
            def at_panel(p, **has):
                step(p, p % 2, {a: (p + a) // 2 + 1 for a in (1, 2)}, **has)

            at_panel(0, post=False, check=True, ahead=True)
            if LOOPS > 1:
                with eng.Fori(0, LOOPS - 1) as i:
                    for c in (1, 2):
                        step(i * 2 + c, c % 2, {a: i + (c + a) // 2 + 1 for a in (1, 2)},
                             post=True, check=True, ahead=True)
            at_panel(P - 3, post=True, check=True, ahead=True)
            at_panel(P - 2, post=True, check=True, ahead=False)
            at_panel(P - 1, post=True, check=False, ahead=False)

        block = ctx.enter_context(nc.Block())

        @block.sync
        def _(sp):
            def load_group(into, src, p, g):
                sp.dma_start(adj_of[into][:, g * TG:(g + 1) * TG, :], src[p, :, g * TG:(g + 1) * TG, :])\
                  .then_inc(slot_in[into][g], 16)

            for g in range(GROUPS):
                load_group(0, t["adj"], 0, g)
            sp.dma_start(x[:, :, :], t["x"]).then_inc(x_in, 16)
            sp.dma_start(xT[:, :], t["xT"][0]).then_inc(xT_in, 16)
            sp.wait_ge(consts_in, 16 * N_CONSTS)
            sp.wait_ge(weights_ready, 2)
            sp.dma_start(brow1[32:35, :], brow1[0:3, :]).then_inc(brow_copied, 16)
            for g in range(GROUPS):
                load_group(1, t["adj"], 1, g)

            def layer1_loads(p, par):
                for g in range(GROUPS):
                    sp.wait_ge(main1, (p - 1) * GROUPS + g + 1)
                    load_group(1 - par, t["adj"], p + 1, g)
                sp.wait_ge(z_done, p * 2)
                sp.dma_start(xT[:, :], t["xT"][p]).then_inc(xT_in, 16)

            panels(sp, layer1_loads)
            for g in range(GROUPS):
                sp.wait_ge(main1, (P - 2) * GROUPS + g + 1)
                load_group(0, t["adj"], 0, g)
            sp.wait_ge(z_done, (P - 1) * 2)
            sp.dma_start(xT[:, :], t["xT"][P - 1]).then_inc(xT_in, 16)
            sp.wait_ge(main1, P * GROUPS)
            for dst, name in ((w_out2, "w_out2"), (w3T, "w3T"), (gamma2, "g2"), (beta2, "be2"), (bias3, "bias3")):
                sp.dma_start(dst[:, :], t[name]).then_inc(consts2_in, 16)

            def layer2_loads(p, par):
                for g in range(GROUPS):
                    sp.wait_ge(main2, (p - 1) * GROUPS + g + 1)
                    load_group(0, t["adj"], p, g)

            panels(sp, layer2_loads)
            layer2_loads(P - 1, 1)
            for g in range(GROUPS):
                sp.wait_ge(main2, (P - 1) * GROUPS + g + 1)
                load_group(0, t["adjT"], 0, g)

            def layer3_loads(p):
                for g in range(GROUPS):
                    sp.wait_ge(w_ready, (p - 1) * PAIRS + (g + 1) * (TG // 2))
                    load_group(0, t["adjT"], p, g)

            def store(p):
                sp.wait_ge(out_ready, p + 1)
                sp.dma_start(t["out"][p], r2[:, :, :]).then_inc(out_stored, 16)

            layer3_loads(1)
            with sp.Fori(0, LOOPS) as i:
                for c in (0, 1):
                    layer3_loads(i * 2 + 2 + c)
                    store(i * 2 + c)
            store(P - 2)
            store(P - 1)
            sp.wait_ge(out_stored, 16 * P)

        @block.gpsimd
        def _(pool):
            gp = nc.gpsimd
            gp.memset(ones[:, :], 1.0).then_inc(pool_consts, 1)
            gp.memset(minus_half[:, :], -0.5).then_inc(pool_consts, 1)
            gp.memset(eps_row[:, :], LN_EPS).then_inc(pool_consts, 1)
            gp.memset(width_row[:, :], float(D)).then_inc(pool_consts, 1)
            gp.memset(ident[:, :], 0.0).then_inc(ident_zero, 1)
            pool.wait_ge(ident_zero, 1)
            gp.affine_select(out=ident[:, :], in_=ident[:, :], compare_op=ALU.not_equal, fill=1.0,
                             base=0, pattern=[[-1, 128]], channel_multiplier=1).then_inc(pool_consts, 1)
            pool.wait_ge(pool_consts, 5)

            def powers1(p):
                link = Links(pool, pool1_links, 2, p)
                for j in range(2):
                    v = slice(2 * j, 2 * j + 2)
                    pool.wait_ge(ln1_stats, p * 2 + j + 1)
                    link(gp.tensor_tensor(out=vtmp[:, v], in0=mv[:, v, 1], in1=eps_row[:, v], op=ALU.add))
                    gp.tensor_tensor(out=rstd[:, v], in0=vtmp[:, v], in1=minus_half[:, v], op=ALU.pow)\
                      .then_inc(rstd1, 1)

            def stage_t2(p):
                gp.tensor_copy(t2s[:, :, :], tc[:, bass.ds(p * B, B), 0:D]).then_inc(t2s_ready, 1)

            def powers2(p):
                link = Links(pool, pool2_links, 3, p)
                pool.wait_ge(ln2_stats, p * 2 + 1)
                link(gp.tensor_tensor(out=vtmp2[:, 0, :], in0=mv2[:, :, 1], in1=eps_row[:, :], op=ALU.add))
                gp.tensor_tensor(out=rstd2[:, 0, :], in0=vtmp2[:, 0, :], in1=minus_half[:, :], op=ALU.pow)\
                  .then_inc(rstd2_ready, 1)
                pool.wait_ge(ln2_stats, p * 2 + 2)
                link(gp.tensor_tensor(out=vtmp2[:, 0, :], in0=mv2[:, :, 1], in1=eps_row[:, :], op=ALU.add))
                link(gp.tensor_tensor(out=vtmp2[:, 1, :], in0=mv2[:, :, 1], in1=width_row[:, :], op=ALU.mult))
                for i in range(2):
                    gp.tensor_tensor(out=rstd2[:, i, :], in0=vtmp2[:, i, :], in1=minus_half[:, :], op=ALU.pow)\
                      .then_inc(rstd2_ready, 1)

            def powers3(p):
                link = Links(pool, pool3_links, 1, p)
                pool.wait_ge(ln3_stats, p + 1)
                link(gp.tensor_tensor(out=vtmp2[:, 0, :], in0=mv2[:, :, 1], in1=eps_row[:, :], op=ALU.add))
                gp.tensor_tensor(out=rstd2[:, 0, :], in0=vtmp2[:, 0, :], in1=minus_half[:, :], op=ALU.pow)\
                  .then_inc(rstd3, 1)

            panels(pool, lambda p, par: powers1(p - 1))
            powers1(P - 2)
            pool.wait_ge(main1, P * GROUPS)
            stage_t2(0)
            powers1(P - 1)

            def layer2_step(p, par):
                pool.wait_ge(main2, p * GROUPS)
                stage_t2(p)
                powers2(p - 1)

            panels(pool, layer2_step)
            layer2_step(P - 1, 1)
            powers2(P - 1)
            panels(pool, lambda p, par: powers3(p - 1))
            powers3(P - 2)
            powers3(P - 1)

        @block.scalar
        def _(act):
            for dst, name in MATRICES:
                act.dma_start(dst[:, :, :], t[name]).then_inc(consts_in, 16)
            for dst, name in ROWS:
                act.dma_start(dst[:, :], t[name]).then_inc(consts_in, 16)
            act.dma_start(bias2[:, 0:D], t["b_in2"]).then_inc(consts_in, 16)
            act.dma_start(bias2[:, D:2 * D], t["b_out2"]).then_inc(consts_in, 16)
            act.dma_start(brow1[1:2, :], t["b_out1"]).then_inc(consts_in, 16)
            act.dma_start(brow1[2:3, :], t["b_self1"]).then_inc(consts_in, 16)

            def signs(p, par, g, which, bias):
                before = p * (4 * GROUPS) + which * (2 * GROUPS) + 2 * g
                src = adj_of[par][:, g * TG:(g + 1) * TG, :].rearrange("p t w -> p (t w)")
                for h in range(2):
                    if not (isinstance(p, int) and p == which == g == h == 0):
                        act.wait_ge(signs_done, before + h)
                    nc.scalar.activation(junk[:, 0:HALF], src[:, h * HALF:(h + 1) * HALF], ACT.Sign, bias=bias,
                                         accum_out=counts[:, which, 2 * g + h:2 * g + h + 1])\
                      .then_inc(signs_done, 1)

            def signs_zero(p, par, g, load):
                act.wait_ge(slot_in[par][g], 16 * load)
                signs(p, par, g, 0, 0.0)

            def relu_hT(p, j):
                act.wait_ge(hT_done, p * 2 + j + 1)
                for h in range(2):
                    last = nc.scalar.activation(h1T[:, h, :, :].rearrange("p b n -> p (b n)"),
                                                big[:, 2, h * 256:(h + 1) * 256], ACT.Relu,
                                                bias=be1c[:, h:h + 1], scale=g1c[:, h:h + 1])
                last.then_inc(h1T_ready, 1)

            def layer1_step(p, par, loads, post, check, ahead):
                if check:
                    for g in (2, 3):
                        signs_zero(p + 1, 1 - par, g, loads[1])
                    act.wait_ge(theta_ready, p + 2)
                    for g in (0, 1):
                        signs(p + 1, 1 - par, g, 1, ntheta[:, 0:1])
                if post:
                    relu_hT(p - 1, 0)
                if check:
                    for g in (2, 3):
                        signs(p + 1, 1 - par, g, 1, ntheta[:, 0:1])
                if post:
                    relu_hT(p - 1, 1)
                if ahead:
                    act.wait_ge(diff_ready, p + 2)
                    for g in (0, 1):
                        signs_zero(p + 2, par, g, loads[2])

            for g in range(GROUPS):
                signs_zero(0, 0, g, 1)
            act.wait_ge(theta_ready, 1)
            for g in range(GROUPS):
                signs(0, 0, g, 1, ntheta[:, 0:1])
            act.wait_ge(diff_ready, 1)
            for g in (0, 1):
                signs_zero(1, 1, g, 1)
            act.wait_ge(consts_in, 16 * N_CONSTS)
            layer1_panels(act, layer1_step)
            for j in range(2):
                relu_hT(P - 1, j)

            def evacuate2(p, par):
                act.wait_ge(main2, p * GROUPS + GROUPS)
                nc.scalar.copy(xs2[:, :], xp[:, par, :]).then_inc(evac2, 1)

            def split_high(p):
                act.wait_ge(uT_done, p + 1)
                nc.scalar.copy(uTh[:, bass.ds(p * W, W)], sm[:, :]).then_inc(uTh_ready, 1)

            def layer2_step(p, par):
                evacuate2(p - 1, 1 - par)
                split_high(p - 1)

            panels(act, layer2_step)
            layer2_step(P - 1, 1)
            act.wait_ge(dve_consts, 3)

            def evacuate3(p, par):
                act.wait_ge(pv_done, p * PAIRS + PAIRS)
                nc.scalar.copy(xs2[:, :], xp[:, par, :]).then_inc(evac3, 1)

            def layer3_step(p, par, first=False):
                for g in range(PAIRS):
                    if first and g == 0:
                        evacuate2(P - 1, 1)
                    if first and g == 2:
                        split_high(P - 1)
                    if not first and g == 3:
                        evacuate3(p - 1, 1 - par)
                    s = big[:, 2 * (g % 2):2 * (g % 2) + 2, :].rearrange("p a w -> p (a w)")
                    act.wait_ge(s_done, p * PAIRS + g + 1)
                    nc.scalar.activation(s, s, ACT.Tanh, scale=b_eighth[:, 0:1]).then_inc(tanh_done, 1)
                    act.wait_ge(tanh_done, p * PAIRS + g + 1)
                    if not (first and g < 2):
                        act.wait_ge(w_ready, p * PAIRS + g - 1)
                    nc.scalar.activation(e[:, g % 2, :], s, ACT.Exp, scale=TANH_RANGE).then_inc(exp_done, 1)

            layer3_step(0, 0, first=True)
            panels(act, layer3_step)
            layer3_step(P - 1, 1)
            evacuate3(P - 1, 1)

        @block.vector
        def _(dve):
            vec = nc.vector

            def carry_wait():
                vec.memset(idle[:, :], 0.0)

            vec.memset(lrow1[:, :], 1.0).then_inc(dve_consts, 1)
            dve.wait_ge(consts_in, 16 * N_CONSTS)
            vec.tensor_scalar(out=b_eighth[:, :], in0=b_eighth[:, :], scalar1=1.0 / TANH_RANGE, scalar2=None,
                              op0=ALU.mult).then_inc(dve_consts, 1)
            vec.tensor_tensor(out=bias2[:, D:2 * D], in0=bias2[:, D:2 * D], in1=b_self2[:, :], op=ALU.add)\
               .then_inc(dve_consts, 1)
            dve.wait_ge(setup_mm, 1)
            vec.tensor_copy(v1[:, :], big[:, 0, 0:H]).then_inc(weights_ready, 1)
            vec.tensor_copy(brow1[0:1, :], big[0:1, 1, 0:H]).then_inc(weights_ready, 1)
            dve.wait_ge(dve_consts, 3)

            def group_sum(p, par, g, load):
                dve.wait_ge(slot_in[par][g], 16 * load)
                src = adj_of[par][:, g * TG:(g + 1) * TG, :].rearrange("p t w -> p w t")
                link = Links(dve, sums_links, 2 * GROUPS - 1, p, before=max(2 * g - 1, 0))
                if g == 0:
                    link(vec.tensor_reduce(out=sums[:, par, :], in_=src, axis=AX.X, op=ALU.add))
                else:
                    link(vec.tensor_reduce(out=part[:, :], in_=src, axis=AX.X, op=ALU.add))
                    link(vec.tensor_tensor(out=sums[:, par, :], in0=sums[:, par, :], in1=part[:, :], op=ALU.add))

            def theta(p):
                link = Links(dve, theta_links, 1, p)
                dve.wait_ge(csum_done, p + 1)
                link(vec.tensor_reduce(out=cmax[:, :], in_=st[:, :], axis=AX.X, op=ALU.max))
                vec.tensor_scalar(out=ntheta[:, :], in0=cmax[:, :], scalar1=EPS, scalar2=-THRESH, op0=ALU.add,
                                  op1=ALU.mult).then_inc(theta_ready, 1)
                vec.tensor_scalar(out=thr[:, :], in0=st[:, :], scalar1=EPS, scalar2=THRESH, op0=ALU.add,
                                  op1=ALU.mult).then_inc(thr_ready, 1)
                dve.wait_ge(thr_ready, p + 1)

            def flag_and_mask(p, par):
                link = Links(dve, flag_links, 3, p)
                dve.wait_ge(signs_done, (p + 1) * (4 * GROUPS))
                d = counts[:, 0, :]
                link(vec.scalar_tensor_tensor(out=d, in0=d, scalar=2.0, in1=counts[:, 1, :],
                                              op0=ALU.mult, op1=ALU.subtract))
                link(vec.tensor_scalar(out=d, in0=d, scalar1=float(-HALF), scalar2=0.0, op0=ALU.add,
                                       op1=ALU.not_equal))
                vec.tensor_reduce(out=cdiff[:, :], in_=d, axis=AX.X, op=ALU.add).then_inc(diff_ready, 1)
                dve.wait_ge(count_done, p + 1)
                link(vec.tensor_scalar(out=flag[:, :], in0=sm[0:1, 8:9], scalar1=1.0, scalar2=None, op0=ALU.min))
                carry_wait()
                flagged = vec.value_load(flag[0:1, 0:1])
                tiles = adj_of[par]
                with dve.If(flagged != 0):
                    with dve.Fori(0, TILES) as k:
                        tile = tiles[:, bass.ds(k, 1), :].rearrange("p a w -> p (a w)")
                        vec.tensor_tensor(out=part[:, :], in0=tile, in1=thr[:, :], op=ALU.is_gt)
                        vec.drain()
                        vec.tensor_tensor(out=tile, in0=tile, in1=part[:, :], op=ALU.mult)
                        vec.drain()
                    vec.tensor_reduce(out=sums[:, par, :], in_=tiles[:, :, :].rearrange("p t w -> p w t"),
                                      axis=AX.X, op=ALU.add)
                    vec.drain()
                vec.engine_nop().then_inc(panel_ready, 1)

            def stats(p, par):
                link = Links(dve, stats_links, 4, p)
                dve.wait_ge(ysum_done, p + 1)
                link(vec.tensor_copy(ysum[:, :], st[:, :]))
                link(vec.scalar_tensor_tensor(out=part[:, :], in0=ysum[:, :], scalar=0.0, in1=ysum[:, :],
                                              op0=ALU.is_le, op1=ALU.add))
                link(vec.scalar_tensor_tensor(out=thr[:, :], in0=thr[:, :], scalar=EPS / THRESH, in1=part[:, :],
                                              op0=ALU.mult, op1=ALU.add))
                link(vec.reciprocal(q[:, :], thr[:, :]))
                rows = slice(32 * par, 32 * par + 1)
                vec.tensor_tensor(out=lrow1[rows, :], in0=q[rows, :], in1=part[rows, :], op=ALU.mult)\
                   .then_inc(stats_ready, 1)
                dve.wait_ge(stats_ready, p + 1)

            def read_cols(p):
                dve.wait_ge(cols_done, p + 1)
                vec.tensor_copy(q_col[:, bass.ds(p * B, B)], sm[:, 0:B]).then_inc(cols_read, 1)
                vec.tensor_scalar(out=no_edge[:, bass.ds(p * B, B)], in0=sm[:, B:2 * B], scalar1=0.0, scalar2=None,
                                  op0=ALU.is_le).then_inc(cols_read, 1)

            def evacuate1(p, par):
                link = Links(dve, evac1_links, 2, p)
                dve.wait_ge(main1, p * GROUPS + GROUPS)
                dve.wait_ge(xT_in, 16 * (p + 1))
                link(vec.scalar_tensor_tensor(out=xs[:, :], in0=ysum[:, :], scalar=0.0, in1=xT[:, :],
                                              op0=ALU.is_le, op1=ALU.mult))
                link(vec.tensor_tensor(out=xs[:, :], in0=xp[:, par, :], in1=xs[:, :], op=ALU.add))
                vec.tensor_tensor(out=xs[:, :], in0=xs[:, :], in1=q[:, :], op=ALU.mult).then_inc(evac1, 1)
                dve.wait_ge(evac1, p + 1)

            def row_stats(link, rows, blocks, into, done):
                for b in blocks:
                    last = vec.bn_stats(bns[:, b, :], rows(b))
                link(last)
                carry_wait()
                for b in blocks:
                    last = vec.bn_aggr(into[:, b, :], bns[:, b, :])
                last.then_inc(done, 1)

            def normalize1(p, j):
                dve.wait_ge(rstd1, p * 2 + j + 1)
                for b in (2 * j, 2 * j + 1):
                    last = vec.tensor_scalar(out=zn[:, b % 2, :], in0=z_of(b), scalar1=mv[:, b, 0:1],
                                             scalar2=rstd[:, b:b + 1], op0=ALU.subtract, op1=ALU.mult)
                last.then_inc(zn_ready, 1)

            def keep_tc(p, j):
                dve.wait_ge(tc_psum, p * 2 + j + 1)
                vec.tensor_tensor(out=tc[:, bass.ds(p * B + 2 * j, 2), :],
                                  in0=big[:, 3, :].rearrange("p (b d) -> p b d", b=2),
                                  in1=bias2[:, :].unsqueeze(1).to_broadcast([128, 2, 2 * D]), op=ALU.add)\
                   .then_inc(tc_ready, 1)

            def norm_and_keep1(p, first_part):
                if first_part:
                    link = Links(dve, ln1_links, 2, p)
                    for j in range(2):
                        dve.wait_ge(z_done, p * 2 + j + 1)
                        row_stats(link, z_of, (2 * j, 2 * j + 1), mv, ln1_stats)
                    normalize1(p, 0)
                else:
                    dve.wait_ge(hT_done, p * 2 + 1)
                    normalize1(p, 1)
                    keep_tc(p, 0)

            def layer1_step(p, par, loads, post, check, ahead):
                if post:
                    evacuate1(p - 1, 1 - par)
                stats(p, par)
                if check:
                    for g in (2, 3):
                        group_sum(p + 1, 1 - par, g, loads[1])
                    theta(p + 1)
                if post:
                    norm_and_keep1(p - 1, True)
                read_cols(p)
                if ahead:
                    group_sum(p + 2, par, 0, loads[2])
                if post:
                    norm_and_keep1(p - 1, False)
                if check:
                    flag_and_mask(p + 1, 1 - par)
                if ahead:
                    group_sum(p + 2, par, 1, loads[2])
                if post:
                    keep_tc(p - 1, 1)

            for g in range(GROUPS):
                group_sum(0, 0, g, 1)
            theta(0)
            flag_and_mask(0, 0)
            for g in (0, 1):
                group_sum(1, 1, g, 1)
            layer1_panels(dve, layer1_step)

            def self_loops(p):
                for b in range(B):
                    last = vec.tensor_scalar(out=loop_d[:, b, :], in0=ident[:, :],
                                             scalar1=no_edge[:, bass.ds(p * B + b, 1)], scalar2=None, op0=ALU.mult)
                last.then_inc(loops_ready, 1)

            def spread(row):
                return row[:, :].unsqueeze(1).to_broadcast([128, B, D])

            def finish2(p):
                here = bass.ds(p * B, B)
                link = Links(dve, ln2_links, 7, p)
                dve.wait_ge(z2_done, p + 1)
                for b in range(B):
                    last = vec.scalar_tensor_tensor(out=r[:, b, :], in0=st4[:, b, :],
                                                    scalar=q_col[:, bass.ds(p * B + b, 1)],
                                                    in1=tc[:, bass.ds(p * B + b, 1), D:2 * D]
                                                    .rearrange("p a d -> p (a d)"),
                                                    op0=ALU.mult, op1=ALU.add)
                link(last)
                row_stats(link, lambda b: r[:, b, :], range(B), mv2, ln2_stats)
                dve.wait_ge(rstd2_ready, p * 3 + 1)
                for b in range(B):
                    last = vec.tensor_scalar(out=r[:, b, :], in0=r[:, b, :], scalar1=mv2[:, b, 0:1],
                                             scalar2=rstd2[:, 0, b:b + 1], op0=ALU.subtract, op1=ALU.mult)
                link(last)
                link(vec.tensor_tensor(out=r[:, :, :], in0=r[:, :, :], in1=spread(gamma2), op=ALU.mult))
                link(vec.tensor_tensor(out=r[:, :, :], in0=r[:, :, :], in1=spread(beta2), op=ALU.add))
                link(vec.scalar_tensor_tensor(out=r[:, :, :], in0=r[:, :, :], scalar=0.0, in1=x[:, here, :],
                                              op0=ALU.max, op1=ALU.add))
                row_stats(link, lambda b: r[:, b, :], range(B), mv2, ln2_stats)
                dve.wait_ge(rstd2_ready, p * 3 + 3)
                for b in range(B):
                    vec.tensor_scalar(out=r2[:, b, :], in0=r[:, b, :], scalar1=mv2[:, b, 0:1],
                                      scalar2=rstd2[:, 1, b:b + 1], op0=ALU.subtract, op1=ALU.mult)
                for b in range(B):
                    last = vec.tensor_scalar(out=x[:, bass.ds(p * B + b, 1), :].rearrange("p a d -> p (a d)"),
                                             in0=r[:, b, :], scalar1=mv2[:, b, 0:1],
                                             scalar2=rstd2[:, 0, b:b + 1], op0=ALU.subtract, op1=ALU.mult)
                last.then_inc(u_ready, 1)
                dve.wait_ge(uTh_ready, p + 1)
                cols = bass.ds(p * W, W)
                vec.tensor_tensor(out=uTl[:, cols], in0=sm[:, :], in1=uTh[:, cols].bitcast(F32), op=ALU.subtract)\
                   .then_inc(uTl_ready, 1)

            evacuate1(P - 1, 1)
            norm_and_keep1(P - 1, True)
            norm_and_keep1(P - 1, False)
            keep_tc(P - 1, 1)
            dve.wait_ge(cols_read, 2 * P)
            self_loops(0)
            dve.wait_ge(consts2_in, 16 * 5)

            def layer2_step(p, par):
                dve.wait_ge(main2, p * GROUPS)
                self_loops(p)
                finish2(p - 1)

            panels(dve, layer2_step)
            layer2_step(P - 1, 1)

            def finish3(p):
                here = bass.ds(p * B, B)
                link = Links(dve, ln3_links, 4, p)
                link(vec.tensor_tensor(out=r[:, :, :], in0=x[:, here, :], in1=spread(bias3), op=ALU.add))
                dve.wait_ge(z3_done, p + 1)
                link(vec.reciprocal(rden[:, :], sm[:, 0:B]))
                for b in range(B):
                    last = vec.scalar_tensor_tensor(out=r[:, b, :], in0=st4[:, b, :], scalar=rden[:, b:b + 1],
                                                    in1=r[:, b, :], op0=ALU.mult, op1=ALU.add)
                link(last)
                row_stats(link, lambda b: r[:, b, :], range(B), mv2, ln3_stats)
                dve.wait_ge(rstd3, p + 1)
                if not (isinstance(p, int) and p == 0):
                    dve.wait_ge(out_stored, 16 * p)
                for b in range(B):
                    last = vec.tensor_scalar(out=r2[:, b, :], in0=r[:, b, :], scalar1=mv2[:, b, 0:1],
                                             scalar2=rstd2[:, 0, b:b + 1], op0=ALU.subtract, op1=ALU.mult)
                last.then_inc(out_ready, 1)
                dve.wait_ge(out_ready, p + 1)

            def add_weights(p, par, g):
                dve.wait_ge(w_ready, p * PAIRS + g + 1)
                if g == 0:
                    vec.tensor_copy(den[:, par, :], pr[:, g % 4, :]).then_inc(den_added, 1)
                else:
                    dve.wait_ge(den_added, p * PAIRS + g)
                    vec.tensor_tensor(out=den[:, par, :], in0=den[:, par, :], in1=pr[:, g % 4, :], op=ALU.add)\
                       .then_inc(den_added, 1)

            def layer3_step(p, par, post, first=False):
                for g in range(PAIRS):
                    if g == FINISH_AT and post is not None:
                        finish3(post)
                    slot = g // (TG // 2)
                    if g % (TG // 2) == 0:
                        dve.wait_ge(slot_in[0][slot], (p + (P // 2 + P + 1)) * 16)
                    dve.wait_ge(exp_done, p * PAIRS + g + 1)
                    if not (first and g < 4):
                        dve.wait_ge(pv_done, p * PAIRS + g - 3)
                    vec.tensor_tensor(out=pr[:, g % 4, :], in0=e[:, g % 2, :],
                                      in1=adjA[:, 2 * g:2 * g + 2, :].rearrange("p a w -> p (a w)"), op=ALU.mult)\
                       .then_inc(w_ready, 1)
                    if g > 0:
                        add_weights(p, par, g - 1)
                add_weights(p, par, PAIRS - 1)

            finish2(P - 1)
            layer3_step(0, 0, None, first=True)
            layer3_step(1, 1, 0)
            with dve.Fori(0, LOOPS) as i:
                layer3_step(i * 2 + 2, 0, i * 2 + 1)
                layer3_step(i * 2 + 3, 1, i * 2 + 2)
            finish3(P - 1)

        @block.tensor
        def _(pe):
            mm = nc.tensor.matmul
            pe.wait_ge(consts_in, 16 * N_CONSTS)
            pe.wait_ge(pool_consts, 5)
            for h in range(2):
                mm(big[:, 0, 0:H], w_in1T[:, h, :], w_out1[:, h, :], start=h == 0, stop=h == 1)
            for h in range(2):
                last = mm(big[0:1, 1, 0:H], b_in1[:, h:h + 1], w_out1[:, h, :], start=h == 0, stop=h == 1)
            last.then_inc(setup_mm, 1)

            def column_sums(p, par):
                pe.wait_ge(sums_links, (2 * GROUPS - 1) * (p + 1))
                mm(st[:, :], ones[:, :], sums[:, par, :], start=True, stop=True).then_inc(csum_done, 1)

            def count(p):
                pe.wait_ge(diff_ready, p + 1)
                mm(sm[0:1, 8:9], cdiff[:, :], ones[:, 0:1], start=True, stop=True).then_inc(count_done, 1)

            def z_products(p, par):
                rows = slice(32 * par, 32 * par + 3)
                pe.wait_ge(evac1, p + 1)
                for b in range(B):
                    cols = slice(b * 128, (b + 1) * 128)
                    mm(z_of(b), xs[:, cols], v1[:, :], start=True, stop=False)
                    mm(z_of(b), xT[:, cols], w_self1[:, :], start=False, stop=False)
                    last = mm(z_of(b), lrow1[rows, cols], brow1[rows, :], start=False, stop=True)
                    if b % 2:
                        last.then_inc(z_done, 1)

            def transposes(p, j):
                pe.wait_ge(zn_ready, p * 2 + j + 1)
                for b in range(2):
                    for h in range(2):
                        last = nc.tensor.transpose(big[:, 2, h * 256 + b * 128:h * 256 + (b + 1) * 128],
                                                   zn[:, b, h * 128:(h + 1) * 128], ident[:, :])
                last.then_inc(hT_done, 1)

            def tc_products(p, j):
                pe.wait_ge(h1T_ready, p * 2 + j + 1)
                if j:
                    pe.wait_ge(tc_ready, p * 2 + 1)
                for b in range(2):
                    for h in range(2):
                        last = mm(big[:, 3, b * 256:(b + 1) * 256], h1T[:, h, b, :], w_cat2[:, h, :],
                                  start=h == 0, stop=h == 1)
                last.then_inc(tc_psum, 1)

            def columns(p):
                pe.wait_ge(stats_ready, p + 1)
                for i, row in enumerate((q, ysum)):
                    for b in range(B):
                        last = mm(sm[:, i * B + b:i * B + b + 1], row[0:1, b * 128:(b + 1) * 128], ones[0:1, 0:1],
                                  start=True, stop=True)
                last.then_inc(cols_done, 1)

            def main(par, src, lhs, g, done):
                for k in range(g * TG, (g + 1) * TG):
                    last = mm(xp[:, par, :], lhs(k), src[:, k, :], start=k == 0, stop=k == TILES - 1)
                last.then_inc(done, 1)

            def layer1_step(p, par, loads, post, check, ahead):
                def main1_group(g):
                    main(par, adj_of[par], lambda k: x[:, k, :], g, main1)

                pe.wait_ge(panel_ready, p + 1)
                mm(st[:, :], ones[:, :], sums[:, par, :], start=True, stop=True).then_inc(ysum_done, 1)
                main1_group(0)
                if post:
                    z_products(p - 1, 1 - par)
                pe.wait_ge(stats_ready, p + 1)
                if check:
                    column_sums(p + 1, 1 - par)
                main1_group(1)
                columns(p)
                if post:
                    transposes(p - 1, 0)
                main1_group(2)
                if post:
                    tc_products(p - 1, 0)
                    transposes(p - 1, 1)
                if check:
                    pe.wait_ge(cols_read, 2 * p + 2)
                    count(p + 1)
                main1_group(3)
                if post:
                    tc_products(p - 1, 1)

            column_sums(0, 0)
            count(0)
            pe.wait_ge(x_in, 16)
            pe.wait_ge(brow_copied, 16)
            layer1_panels(pe, layer1_step)

            def main2_group(p, par, g):
                pe.wait_ge(slot_in[0][g], (p + (P // 2 + 1)) * 16)
                if g == GROUPS - 1:
                    pe.wait_ge(t2s_ready, p + 1)
                    pe.wait_ge(loops_ready, p + 1)
                    for b in range(B):
                        mm(xp[:, par, b * 128:(b + 1) * 128], t2s[:, b, :], loop_d[:, b, :], start=False, stop=False)
                main(par, adjA, lambda k: tc[:, k, 0:D], g, main2)

            def z2_products(p):
                pe.wait_ge(evac2, p + 1)
                for b in range(B):
                    last = mm(st4[:, b, :], xs2[:, b * 128:(b + 1) * 128], w_out2[:, :], start=True, stop=True)
                last.then_inc(z2_done, 1)

            def u_transposes(p):
                pe.wait_ge(u_ready, p + 1)
                for b in range(B):
                    last = nc.tensor.transpose(sm[:, b * 128:(b + 1) * 128], r2[:, b, :], ident[:, :])
                last.then_inc(uT_done, 1)

            def rows_known(g):
                pe.wait_ge(tc_ready, 2 * (((g + 1) * TG + B - 1) // B))

            rows_known(0)
            main2_group(0, 0, 0)
            z_products(P - 1, 1)
            if GROUPS * B < TILES:
                rows_known(1)
                main2_group(0, 0, 1)
            transposes(P - 1, 0)
            if GROUPS * B < TILES:
                rows_known(2)
                main2_group(0, 0, 2)
            tc_products(P - 1, 0)
            transposes(P - 1, 1)
            tc_products(P - 1, 1)
            for g in (range(3, 4) if GROUPS * B < TILES else range(1, 4)):
                rows_known(g)
                main2_group(0, 0, g)
            pe.wait_ge(consts2_in, 16 * 5)

            def layer2_step(p, par):
                main2_group(p, par, 0)
                z2_products(p - 1)
                main2_group(p, par, 1)
                main2_group(p, par, 2)
                u_transposes(p - 1)
                main2_group(p, par, 3)

            panels(pe, layer2_step)
            layer2_step(P - 1, 1)

            def scores(p, g, first):
                if first:
                    pe.wait_ge(uTl_ready, (2 * g + 1) // B + 1)
                if not (first and g < 2):
                    pe.wait_ge(exp_done, p * PAIRS + g - 1)
                cols = bass.ds(p * W, W)
                for k in range(2):
                    tile = slice((2 * g + k) * 128, (2 * g + k + 1) * 128)
                    s = big[:, 2 * (g % 2) + k, :]
                    mm(s, uTh[:, tile], uTh[:, cols], start=True, stop=False)
                    mm(s, uTh[:, tile], uTl[:, cols], start=False, stop=False)
                    last = mm(s, uTl[:, tile], uTh[:, cols], start=False, stop=True)
                last.then_inc(s_done, 1)

            def weighted(p, par, g):
                pe.wait_ge(w_ready, p * PAIRS + g + 1)
                for k in range(2):
                    last = mm(xp[:, par, :], x[:, 2 * g + k, :], pr[:, g % 4, k * W:(k + 1) * W],
                              start=g == 0 and k == 0, stop=g == PAIRS - 1 and k == 1)
                last.then_inc(pv_done, 1)

            def z3_products(p, par):
                pe.wait_ge(evac3, p + 1)
                for b in range(B):
                    mm(st4[:, b, :], xs2[:, b * 128:(b + 1) * 128], w3T[:, :], start=True, stop=True)
                pe.wait_ge(den_added, (p + 1) * PAIRS)
                for b in range(B):
                    for k in range(2):
                        last = mm(sm[:, b:b + 1], den[:, par, k * W + b * 128:k * W + (b + 1) * 128], ones[:, 0:1],
                                  start=k == 0, stop=k == 1)
                last.then_inc(z3_done, 1)

            def layer3_step(p, par, first=False):
                for g in range(PAIRS):
                    if first and g == 0:
                        z2_products(P - 1)
                    if first and g == 2:
                        u_transposes(P - 1)
                    scores(p, g, first)
                    if g >= 2:
                        weighted(p, par, g - 2)
                    elif not first:
                        weighted(p - 1, 1 - par, PAIRS - 2 + g)
                    if g == Z3_AT and not first:
                        z3_products(p - 1, 1 - par)

            layer3_step(0, 0, first=True)
            panels(pe, layer3_step)
            layer3_step(P - 1, 1)
            for g in (PAIRS - 2, PAIRS - 1):
                weighted(P - 1, 1, g)
            z3_products(P - 1, 1)


Z3_AT = 4
FINISH_AT = 5


def run_kernel_program(nc, tensors):
    build_program(nc, tensors)


def layouts(i):
    import numpy as np

    def blocks(a):
        return a.reshape(-1, 128, a.shape[1]).transpose(1, 0, 2)

    def panels_of(a):
        n = a.shape[0]
        return a.reshape(n // 128, 128, n // W, W).transpose(2, 1, 0, 3)

    def over_partitions(a):
        return np.broadcast_to(a.reshape(1, -1), (128, a.size))

    x, adj = i["x"], i["adj"]
    n = x.shape[0]
    out = {
        "x": blocks(x),
        "xT": x.T.reshape(x.shape[1], n // W, W).transpose(1, 0, 2),
        "adj": panels_of(adj),
        "adjT": panels_of(adj.T),
        "w_in1T": blocks(i["L0_gnn_W_in1"].T),
        "w_out1": blocks(i["L0_gnn_W_out1"]),
        "w_self1": i["L0_gnn_W_self1"],
        "b_in1": i["L0_gnn_b_in1"].reshape(2, 128).T,
        "b_out1": i["L0_gnn_b_out1"].reshape(1, -1),
        "b_self1": i["L0_gnn_b_self1"].reshape(1, -1),
        "g1": i["L0_gnn_g1"].reshape(2, 128).T,
        "be1": i["L0_gnn_be1"].reshape(2, 128).T,
        "w_cat2": blocks(np.concatenate([i["L0_gnn_W_in2"], i["L0_gnn_W_self2"]], axis=1)),
        "b_in2": over_partitions(i["L0_gnn_b_in2"]),
        "b_out2": over_partitions(i["L0_gnn_b_out2"]),
        "b_self2": over_partitions(i["L0_gnn_b_self2"]),
        "w_out2": i["L0_gnn_W_out2"],
        "g2": over_partitions(i["L0_gnn_g2"]),
        "be2": over_partitions(i["L0_gnn_be2"]),
        "w3T": i["L1_gnn_W"].T,
        "bias3": over_partitions(i["L1_gnn_bias"]),
        "b": over_partitions(i["L1_gnn_b"]),
    }
    return {k: np.ascontiguousarray(v) for k, v in out.items()}


def kernel(**inputs):
    import numpy as np
    import concourse.bacc as bacc
    from concourse.bass_utils import run_bass_kernel_spmd

    arrays = layouts({k: np.asarray(v) for k, v in inputs.items()})
    n, d = np.asarray(inputs["x"]).shape
    nc = bacc.Bacc("TRN2", target_bir_lowering=False, num_devices=1)
    tensors = {k: nc.dram_tensor(f"in_{k}", a.shape, mybir.dt.from_np(a.dtype), kind="ExternalInput").ap()
               for k, a in arrays.items()}
    tensors["out"] = nc.dram_tensor("out_rows", (n // W, 128, B, d), F32, kind="ExternalOutput").ap()
    build_program(nc, tensors)
    result = run_bass_kernel_spmd(nc, [{f"in_{k}": a for k, a in arrays.items()}], core_ids=[0])
    rows = result.results[0]["out_rows"]
    return rows.transpose(0, 2, 1, 3).reshape(n, d)
```

```python
from contextlib import ExitStack

import concourse.bass as bass
from concourse import mybir

F32 = mybir.dt.float32
F32R = mybir.dt.float32r
I8 = mybir.dt.int8
I32 = mybir.dt.int32
ALU = mybir.AluOpType
ACT = mybir.ActivationFunctionType
AX = mybir.AxisListType

THRESH = 1e-6
EPS = 1e-8
LN_EPS = 1e-5
TANH_RANGE = 8.0

W = 512
B = W // 128
GROUPS = 4
SBUF_START = 16512
SBUF_END = 229344
KIB = 1024


class Links:

    def __init__(self, eng, sem, count, panel, before=0):
        self.eng, self.sem, self.first, self.n = eng, sem, panel * count, before

    def __call__(self, ins):
        ins.then_inc(self.sem, 1)
        self.n += 1
        self.eng.wait_ge(self.sem, self.first + self.n)


def build_program(nc, t):
    NB = t["x"].shape[1]
    TILES = NB
    N = NB * 128
    P = N // W
    TG = TILES // GROUPS
    PAIRS = TILES // 2
    LOOPS = (P - 2) // 2
    D, H = 128, 256
    HALF = TG * W // 2
    BOUND = 1.001 * THRESH * N

    ctx = ExitStack()
    with ctx:
        place = [SBUF_START]

        def at(name, shape, dt=F32, offset=None):
            size = 1 if dt == I8 else 4
            for s in shape[1:]:
                size *= s
            if offset is None:
                offset = place[0]
                place[0] += (size + 31) // 32 * 32
            return nc.alloc_sbuf_tensor_at(name, shape, dt, offset=offset)

        def sem(name):
            return ctx.enter_context(nc.semaphore(name))

        adjA = at("adjA", [128, TILES, W])
        b_start = place[0]
        adjB = at("adjB", [128, TILES, W])
        b_end = place[0] = b_start + 64 * KIB
        adj_of = (adjA, adjB)
        x = at("x_nodes", [128, NB, D])
        tc_start = place[0]
        tc = at("t2_self2", [128, NB, 2 * D])
        ident = at("ident", [128, 128])
        ones = at("ones", [128, 128])
        layer1_start = place[0]
        xT = at("xT_panel", [128, W])
        w_self1 = at("w_self1_sb", [128, H])
        w_cat2 = at("w_in2_self2", [128, 2, 2 * D])
        v1 = at("w_in1_w_out1", [128, H])
        brow1 = at("bias_rows1", [35, H])
        lrow1 = at("bias_left1", [35, W])
        bias2 = at("bias2", [128, 2 * D])
        sums = at("column_sums", [128, 2, W])
        part = at("part_sums", [128, W])
        thr = at("thresholds", [128, W])
        ysum = at("edge_sums", [128, W])
        q = at("q_row", [128, W])
        xs = at("scaled_x", [128, W])
        zn = at("z_normed", [128, 2, H])
        h1T = at("h1T", [128, 2, 2, 128])
        junk = at("sign_out", [128, 2048], I8)
        layer1_end = place[0]
        g1c = at("gamma1", [128, 2])
        be1c = at("beta1", [128, 2])
        q_col = at("q_col", [128, NB])
        no_edge = at("no_edge", [128, NB])
        minus_half = at("minus_half", [128, B])
        eps_row = at("eps_row", [128, B])
        width_row = at("width_row", [128, B])
        counts = at("sign_counts", [128, 2, 2, 2 * GROUPS])
        flag = at("flag", [1, 1], I32)
        bns = at("bn_stats_out", [128, B, 6])
        mv = at("mean_var", [128, B, 2])
        vtmp = at("var_tmp", [128, B])
        rstd = at("rstd", [128, B])
        scalars = at("scalars", [128, 4])
        cmax, cdiff, minus_bound, b_eighth = (scalars[:, i:i + 1] for i in range(4))
        idle = at("idle", [1, 1])
        assert place[0] <= SBUF_END, place[0]
        w_in1T = at("w_in1T_sb", [128, 2, D], offset=tc_start)
        w_out1 = at("w_out1_sb", [128, 2, H], offset=tc_start + KIB)
        b_in1 = at("b_in1_sb", [128, 2], offset=tc_start + 3 * KIB)
        b_self2 = at("b_self2_sb", [128, D], offset=tc_start + 4 * KIB)
        place[0] = b_start
        uTh = at("uT_high", [128, N], F32R)
        uTl = at("uT_low", [128, N], F32R)
        w3 = at("w3T_sb", [128, D])
        w3_last = at("w3T_last_row", [128, D])
        bias3 = at("bias3_sb", [128, D])
        xs2 = at("x_out", [128, W])
        r = at("rows", [128, B, D])
        r2 = at("rows_out", [128, B, D])
        mv2 = at("mean_var2", [128, B, 2])
        vtmp2 = at("var_tmp2", [128, 2, B])
        rstd2 = at("rstd2", [128, 2, B])
        rden = at("inv_weight_sum", [128, B])
        layer2_start = place[0]
        w_out2 = at("w_out2_sb", [128, D])
        gamma2 = at("gamma2", [128, D])
        beta2 = at("beta2", [128, D])
        loop_d = at("self_loops", [128, B, 128])
        t2s = at("t2_blocks", [128, B, D])
        assert place[0] <= b_end, (place[0], b_end)
        place[0] = layer2_start
        pw = at("weights3", [128, 2, 2 * W])
        ph = at("weights3_high", [128, 4, 2 * W], F32R)
        assert place[0] <= b_end, (place[0], b_end)
        place[0] = layer1_start
        pl = at("weights3_low", [128, 4, 2 * W], F32R)
        e = at("exp_out", [128, 2, 2 * W])
        assert place[0] <= layer1_end, (place[0], layer1_end)
        xh = at("x_high", [128, NB, D], F32R, offset=tc_start)
        xl = at("x_low", [128, NB, D], F32R, offset=tc_start + N * D * 4 // 128)

        xp = ctx.enter_context(nc.psum_tensor("xp", [128, 2, W], F32))
        st = ctx.enter_context(nc.psum_tensor("st", [128, W], F32))
        sm = ctx.enter_context(nc.psum_tensor("sm", [128, W], F32))
        big = ctx.enter_context(nc.psum_tensor("big", [128, 4, W], F32))
        st4 = st[:, :].rearrange("p (b d) -> p b d", b=B)

        def z_of(b):
            return big[:, b // 2, (b % 2) * H:(b % 2 + 1) * H]

        slot_in = [[sem(f"slot_in{i}{g}") for g in range(GROUPS)] for i in range(2)]
        x_in = sem("x_in")
        xT_in = sem("xT_in")
        consts_in = sem("consts_in")
        consts2_in = sem("consts2_in")
        brow_copied = sem("brow_copied")
        ident_zero = sem("ident_zero")
        pool_consts = sem("pool_consts")
        dve_consts = sem("dve_consts")
        setup_mm = sem("setup_mm")
        weights_ready = sem("weights_ready")
        sums_links = sem("sums_links")
        csum_done = sem("csum_done")
        thr_ready = sem("thr_ready")
        signs_done = sem("signs_done")
        diff_links = sem("diff_links")
        flag_links = sem("flag_links")
        diff_ready = sem("diff_ready")
        count_done = sem("count_done")
        panel_ready = sem("panel_ready")
        ysum_done = sem("ysum_done")
        stats_links = sem("stats_links")
        ysum_read = sem("ysum_read")
        q_links = sem("q_links")
        q_ready = sem("q_ready")
        cols_done = sem("cols_done")
        cols_read = sem("cols_read")
        main1 = sem("main1_group")
        evac1_links = sem("evac1_links")
        evac1 = sem("evac1_done")
        z_done = sem("z_done")
        ln1_links = sem("ln1_links")
        ln1_stats = sem("ln1_stats")
        pool1_links = sem("pool1_links")
        rstd1 = sem("rstd1_ready")
        zn_ready = sem("zn_ready")
        hT_done = sem("hT_done")
        h1T_ready = sem("h1T_ready")
        tc_psum = sem("tc_psum_done")
        tc_ready = sem("tc_ready")
        main2 = sem("main2_group")
        loops_ready = sem("loops_ready")
        t2s_ready = sem("t2s_ready")
        evac2 = sem("evac2_done")
        z2_done = sem("z2_done")
        ln2_links = sem("ln2_links")
        ln2_stats = sem("ln2_stats")
        pool2_links = sem("pool2_links")
        rstd2_ready = sem("rstd2_ready")
        u_ready = sem("u_ready")
        uT_done = sem("uT_psum_done")
        uTh_ready = sem("uTh_ready")
        uTl_ready = sem("uTl_ready")
        s_done = sem("s_done")
        tanh_done = sem("tanh_done")
        exp_done = sem("exp_done")
        w_ready = sem("w_ready")
        ph_ready = sem("ph_ready")
        ph_dve = sem("ph_dve")
        pl_ready = sem("pl_ready")
        w3_ready = sem("w3_ready")
        x_last_ready = sem("x_last_ready")
        xh_ready = sem("xh_ready")
        xl_ready = sem("xl_ready")
        pv_done = sem("pv_done")
        evac3 = sem("evac3_done")
        z3_done = sem("z3_done")
        ln3_links = sem("ln3_links")
        ln3_stats = sem("ln3_stats")
        pool3_links = sem("pool3_links")
        rstd3 = sem("rstd3_ready")
        out_ready = sem("out_ready")
        out_stored = sem("out_stored")

        MATRICES = ((w_in1T, "w_in1T"), (w_out1, "w_out1"), (w_cat2, "w_cat2"))
        ROWS = ((b_in1, "b_in1"), (w_self1, "w_self1"), (g1c, "g1"), (be1c, "be1"), (b_self2, "b_self2"),
                (b_eighth, "b"))
        CONSTS2 = ((w_out2, "w_out2"), (w3, "w3T"), (w3_last, "w3T_last"), (gamma2, "g2"), (beta2, "be2"),
                   (bias3, "bias3"))
        N_CONSTS = len(MATRICES) + len(ROWS) + 4

        def panels(eng, step):
            with eng.Fori(0, LOOPS) as i:
                step(i * 2 + 1, 1)
                step(i * 2 + 2, 0)

        def layer1_panels(eng, step):
            def at_panel(p, **has):
                step(p, p % 2, {a: (p + a) // 2 + 1 for a in (1, 2)}, **has)

            at_panel(0, post=False, check=True, ahead=True)
            if LOOPS > 1:
                with eng.Fori(0, LOOPS - 1) as i:
                    for c in (1, 2):
                        step(i * 2 + c, c % 2, {a: i + (c + a) // 2 + 1 for a in (1, 2)},
                             post=True, check=True, ahead=True)
            at_panel(P - 3, post=True, check=True, ahead=True)
            at_panel(P - 2, post=True, check=True, ahead=False)
            at_panel(P - 1, post=True, check=False, ahead=False)

        block = ctx.enter_context(nc.Block())

        @block.sync
        def _(sp):
            def load_group(into, src, p, g):
                sp.dma_start(adj_of[into][:, g * TG:(g + 1) * TG, :], src[p, :, g * TG:(g + 1) * TG, :])\
                  .then_inc(slot_in[into][g], 16)

            load_group(0, t["adj"], 0, 0)
            sp.wait_ge(consts_in, 16 * N_CONSTS)
            for g in range(1, GROUPS):
                load_group(0, t["adj"], 0, g)
            sp.dma_start(x[:, :, :], t["x"]).then_inc(x_in, 16)
            sp.dma_start(xT[:, :], t["xT"][0]).then_inc(xT_in, 16)
            for g in range(GROUPS):
                load_group(1, t["adj"], 1, g)
            sp.wait_ge(weights_ready, 2)
            sp.dma_start(brow1[32:35, :], brow1[0:3, :]).then_inc(brow_copied, 16)

            def layer1_loads(p, par):
                for g in range(GROUPS):
                    sp.wait_ge(main1, (p - 1) * GROUPS + g + 1)
                    load_group(1 - par, t["adj"], p + 1, g)
                sp.wait_ge(z_done, p * 2)
                sp.dma_start(xT[:, :], t["xT"][p]).then_inc(xT_in, 16)

            panels(sp, layer1_loads)
            for g in range(GROUPS):
                sp.wait_ge(main1, (P - 2) * GROUPS + g + 1)
                load_group(0, t["adj"], 0, g)
            sp.wait_ge(z_done, (P - 1) * 2)
            sp.dma_start(xT[:, :], t["xT"][P - 1]).then_inc(xT_in, 16)
            sp.wait_ge(main1, P * GROUPS)
            for dst, name in CONSTS2:
                sp.dma_start(dst[:, :], t[name]).then_inc(consts2_in, 16)

            def layer2_loads(p, par):
                for g in range(GROUPS):
                    sp.wait_ge(main2, (p - 1) * GROUPS + g + 1)
                    load_group(0, t["adj"], p, g)

            panels(sp, layer2_loads)
            layer2_loads(P - 1, 1)
            for g in range(GROUPS):
                sp.wait_ge(main2, (P - 1) * GROUPS + g + 1)
                load_group(0, t["adjT"], 0, g)

            def layer3_loads(p):
                for g in range(GROUPS):
                    sp.wait_ge(w_ready, (p - 1) * PAIRS + (g + 1) * (TG // 2))
                    load_group(0, t["adjT"], p, g)

            def store(p):
                sp.wait_ge(out_ready, p + 1)
                sp.dma_start(t["out"][p], r2[:, :, :]).then_inc(out_stored, 16)

            layer3_loads(1)
            with sp.Fori(0, LOOPS) as i:
                for c in (0, 1):
                    layer3_loads(i * 2 + 2 + c)
                    store(i * 2 + c)
            store(P - 2)
            store(P - 1)
            sp.wait_ge(out_stored, 16 * P)

        @block.gpsimd
        def _(pool):
            gp = nc.gpsimd
            gp.memset(minus_bound[:, :], -BOUND).then_inc(pool_consts, 1)
            gp.memset(ones[:, :], 1.0).then_inc(pool_consts, 1)
            gp.memset(minus_half[:, :], -0.5).then_inc(pool_consts, 1)
            gp.memset(eps_row[:, :], LN_EPS).then_inc(pool_consts, 1)
            gp.memset(width_row[:, :], float(D)).then_inc(pool_consts, 1)
            gp.memset(ident[:, :], 0.0).then_inc(ident_zero, 1)
            pool.wait_ge(ident_zero, 1)
            gp.affine_select(out=ident[:, :], in_=ident[:, :], compare_op=ALU.not_equal, fill=1.0,
                             base=0, pattern=[[-1, 128]], channel_multiplier=1).then_inc(pool_consts, 1)
            pool.wait_ge(pool_consts, 6)

            def powers1(p):
                link = Links(pool, pool1_links, 2, p)
                for j in range(2):
                    v = slice(2 * j, 2 * j + 2)
                    pool.wait_ge(ln1_stats, p * 2 + j + 1)
                    link(gp.tensor_tensor(out=vtmp[:, v], in0=mv[:, v, 1], in1=eps_row[:, v], op=ALU.add))
                    gp.tensor_tensor(out=rstd[:, v], in0=vtmp[:, v], in1=minus_half[:, v], op=ALU.pow)\
                      .then_inc(rstd1, 1)

            def stage_t2(p):
                gp.tensor_copy(t2s[:, :, :], tc[:, bass.ds(p * B, B), 0:D]).then_inc(t2s_ready, 1)

            def powers2(p):
                link = Links(pool, pool2_links, 3, p)
                pool.wait_ge(ln2_stats, p * 2 + 1)
                link(gp.tensor_tensor(out=vtmp2[:, 0, :], in0=mv2[:, :, 1], in1=eps_row[:, :], op=ALU.add))
                gp.tensor_tensor(out=rstd2[:, 0, :], in0=vtmp2[:, 0, :], in1=minus_half[:, :], op=ALU.pow)\
                  .then_inc(rstd2_ready, 1)
                pool.wait_ge(ln2_stats, p * 2 + 2)
                link(gp.tensor_tensor(out=vtmp2[:, 0, :], in0=mv2[:, :, 1], in1=eps_row[:, :], op=ALU.add))
                link(gp.tensor_tensor(out=vtmp2[:, 1, :], in0=mv2[:, :, 1], in1=width_row[:, :], op=ALU.mult))
                for i in range(2):
                    gp.tensor_tensor(out=rstd2[:, i, :], in0=vtmp2[:, i, :], in1=minus_half[:, :], op=ALU.pow)\
                      .then_inc(rstd2_ready, 1)

            def powers3(p):
                link = Links(pool, pool3_links, 1, p)
                pool.wait_ge(ln3_stats, p + 1)
                link(gp.tensor_tensor(out=vtmp2[:, 0, :], in0=mv2[:, :, 1], in1=eps_row[:, :], op=ALU.add))
                gp.tensor_tensor(out=rstd2[:, 0, :], in0=vtmp2[:, 0, :], in1=minus_half[:, :], op=ALU.pow)\
                  .then_inc(rstd3, 1)

            panels(pool, lambda p, par: powers1(p - 1))
            powers1(P - 2)
            pool.wait_ge(main1, P * GROUPS)
            stage_t2(0)
            powers1(P - 1)

            def layer2_step(p, par):
                pool.wait_ge(main2, p * GROUPS)
                stage_t2(p)
                powers2(p - 1)

            panels(pool, layer2_step)
            layer2_step(P - 1, 1)
            powers2(P - 1)
            panels(pool, lambda p, par: powers3(p - 1))
            powers3(P - 2)
            powers3(P - 1)

        @block.scalar
        def _(act):
            for dst, name in MATRICES:
                act.dma_start(dst[:, :, :], t[name]).then_inc(consts_in, 16)
            for dst, name in ROWS:
                act.dma_start(dst[:, :], t[name]).then_inc(consts_in, 16)
            act.dma_start(bias2[:, 0:D], t["b_in2"]).then_inc(consts_in, 16)
            act.dma_start(bias2[:, D:2 * D], t["b_out2"]).then_inc(consts_in, 16)
            act.dma_start(brow1[1:2, :], t["b_out1"]).then_inc(consts_in, 16)
            act.dma_start(brow1[2:3, :], t["b_self1"]).then_inc(consts_in, 16)

            def signs(p, par, g, load, halves=(0, 1)):
                act.wait_ge(slot_in[par][g], 16 * load)
                src = adj_of[par][:, g * TG:(g + 1) * TG, :].rearrange("p t w -> p (t w)")
                for h in halves:
                    for which, bias in ((0, 0.0), (1, minus_bound[:, 0:1])):
                        n = 4 * g + 2 * h + which
                        if not (isinstance(p, int) and p == n == 0):
                            act.wait_ge(signs_done, p * (4 * GROUPS) + n)
                        nc.scalar.activation(junk[:, 0:HALF], src[:, h * HALF:(h + 1) * HALF], ACT.Sign, bias=bias,
                                             accum_out=counts[:, par, which, 2 * g + h:2 * g + h + 1])\
                          .then_inc(signs_done, 1)

            def relu_hT(p, j):
                act.wait_ge(hT_done, p * 2 + j + 1)
                for h in range(2):
                    last = nc.scalar.activation(h1T[:, h, :, :].rearrange("p b n -> p (b n)"),
                                                big[:, 2, h * 256:(h + 1) * 256], ACT.Relu,
                                                bias=be1c[:, h:h + 1], scale=g1c[:, h:h + 1])
                last.then_inc(h1T_ready, 1)

            def layer1_step(p, par, loads, post, check, ahead):
                if check:
                    for g in (2, 3):
                        signs(p + 1, 1 - par, g, loads[1])
                if ahead:
                    act.wait_ge(diff_ready, p + 1)
                    signs(p + 2, par, 0, loads[2], (0,))
                if post:
                    relu_hT(p - 1, 0)
                if ahead:
                    signs(p + 2, par, 0, loads[2], (1,))
                    signs(p + 2, par, 1, loads[2], (0,))
                if post:
                    relu_hT(p - 1, 1)
                if ahead:
                    signs(p + 2, par, 1, loads[2], (1,))

            act.wait_ge(pool_consts, 1)
            for g in range(GROUPS):
                signs(0, 0, g, 1)
            for g in (0, 1):
                signs(1, 1, g, 1)
            act.wait_ge(consts_in, 16 * N_CONSTS)
            layer1_panels(act, layer1_step)
            for j in range(2):
                relu_hT(P - 1, j)

            def evacuate2(p, par):
                act.wait_ge(main2, p * GROUPS + GROUPS)
                nc.scalar.copy(xs2[:, :], xp[:, par, :]).then_inc(evac2, 1)

            def split_high(p):
                act.wait_ge(uT_done, p + 1)
                nc.scalar.copy(uTh[:, bass.ds(p * W, W)], sm[:, :]).then_inc(uTh_ready, 1)

            def layer2_step(p, par):
                evacuate2(p - 1, 1 - par)
                split_high(p - 1)

            panels(act, layer2_step)
            layer2_step(P - 1, 1)
            act.wait_ge(dve_consts, 3)

            def evacuate3(p, par):
                act.wait_ge(pv_done, p * PAIRS + PAIRS)
                nc.scalar.copy(xs2[:, :], xp[:, par, :]).then_inc(evac3, 1)

            def weights_high(p, g):
                act.wait_ge(w_ready, p * PAIRS + g + 1)
                if not (isinstance(p, int) and p == 0 and g < 4):
                    act.wait_ge(pv_done, p * PAIRS + g - 3)
                nc.scalar.copy(ph[:, g % 4, :], pw[:, g % 2, :]).then_inc(ph_ready, 1)

            def layer3_step(p, par, first=False):
                for g in range(PAIRS):
                    if first and g == 0:
                        evacuate2(P - 1, 1)
                    if first and g == 1:
                        split_high(P - 1)
                    if not first and g == 4:
                        evacuate3(p - 1, 1 - par)
                    s = big[:, 2 * (g % 2):2 * (g % 2) + 2, :].rearrange("p a w -> p (a w)")
                    act.wait_ge(s_done, p * PAIRS + g + 1)
                    nc.scalar.activation(s, s, ACT.Tanh, scale=b_eighth[:, 0:1]).then_inc(tanh_done, 1)
                    act.wait_ge(tanh_done, p * PAIRS + g + 1)
                    if not (first and g < 2):
                        act.wait_ge(w_ready, p * PAIRS + g - 1)
                    nc.scalar.activation(e[:, g % 2, :], s, ACT.Exp, scale=TANH_RANGE).then_inc(exp_done, 1)
                    if g == 0:
                        if not first:
                            weights_high(p - 1, PAIRS - 1)
                    elif g - 1 not in HIGH_ON_DVE:
                        weights_high(p, g - 1)

            layer3_step(0, 0, first=True)
            panels(act, layer3_step)
            layer3_step(P - 1, 1)
            weights_high(P - 1, PAIRS - 1)
            evacuate3(P - 1, 1)

        @block.vector
        def _(dve):
            vec = nc.vector

            def carry_wait():
                vec.memset(idle[:, :], 0.0)

            vec.memset(lrow1[:, :], 1.0).then_inc(dve_consts, 1)

            def setup():
                dve.wait_ge(consts_in, 16 * N_CONSTS)
                vec.tensor_scalar(out=b_eighth[:, :], in0=b_eighth[:, :], scalar1=1.0 / TANH_RANGE, scalar2=None,
                                  op0=ALU.mult).then_inc(dve_consts, 1)
                vec.tensor_tensor(out=bias2[:, D:2 * D], in0=bias2[:, D:2 * D], in1=b_self2[:, :], op=ALU.add)\
                   .then_inc(dve_consts, 1)
                dve.wait_ge(setup_mm, 1)
                vec.tensor_copy(v1[:, :], big[:, 0, 0:H]).then_inc(weights_ready, 1)
                vec.tensor_copy(brow1[0:1, :], big[0:1, 1, 0:H]).then_inc(weights_ready, 1)
                dve.wait_ge(dve_consts, 3)

            def group_sum(p, par, g, load):
                dve.wait_ge(slot_in[par][g], 16 * load)
                src = adj_of[par][:, g * TG:(g + 1) * TG, :].rearrange("p t w -> p w t")
                link = Links(dve, sums_links, 2 * GROUPS - 1, p, before=max(2 * g - 1, 0))
                if g == 0:
                    link(vec.tensor_reduce(out=sums[:, par, :], in_=src, axis=AX.X, op=ALU.add))
                else:
                    link(vec.tensor_reduce(out=part[:, :], in_=src, axis=AX.X, op=ALU.add))
                    link(vec.tensor_tensor(out=sums[:, par, :], in0=sums[:, par, :], in1=part[:, :], op=ALU.add))

            def thresholds(p):
                dve.wait_ge(csum_done, p + 1)
                vec.tensor_reduce(out=cmax[:, :], in_=st[:, :], axis=AX.X, op=ALU.max).then_inc(thr_ready, 1)
                vec.tensor_scalar(out=thr[:, :], in0=st[:, :], scalar1=EPS, scalar2=THRESH, op0=ALU.add,
                                  op1=ALU.mult).then_inc(thr_ready, 1)
                dve.wait_ge(thr_ready, 2 * p + 2)

            def compare(p, par):
                link = Links(dve, diff_links, 3, p)
                dve.wait_ge(signs_done, (p + 1) * (4 * GROUPS))
                d = counts[:, par, 0, :]
                link(vec.scalar_tensor_tensor(out=d, in0=d, scalar=2.0, in1=counts[:, par, 1, :],
                                              op0=ALU.mult, op1=ALU.subtract))
                link(vec.tensor_scalar(out=d, in0=d, scalar1=float(-HALF), scalar2=0.0, op0=ALU.add,
                                       op1=ALU.not_equal))
                link(vec.tensor_reduce(out=cdiff[:, :], in_=d, axis=AX.X, op=ALU.add))
                vec.scalar_tensor_tensor(out=cdiff[:, :], in0=cmax[:, :], scalar=float(N), in1=cdiff[:, :],
                                         op0=ALU.is_gt, op1=ALU.add).then_inc(diff_ready, 1)

            def mask(p, par):
                link = Links(dve, flag_links, 1, p)
                dve.wait_ge(count_done, p + 1)
                link(vec.tensor_scalar(out=flag[:, :], in0=sm[0:1, 8:9], scalar1=1.0, scalar2=None, op0=ALU.min))
                carry_wait()
                flagged = vec.value_load(flag[0:1, 0:1])
                tiles = adj_of[par]
                with dve.If(flagged != 0):
                    with dve.Fori(0, TILES) as k:
                        tile = tiles[:, bass.ds(k, 1), :].rearrange("p a w -> p (a w)")
                        vec.tensor_tensor(out=part[:, :], in0=tile, in1=thr[:, :], op=ALU.is_gt)
                        vec.drain()
                        vec.tensor_tensor(out=tile, in0=tile, in1=part[:, :], op=ALU.mult)
                        vec.drain()
                    vec.tensor_reduce(out=sums[:, par, :], in_=tiles[:, :, :].rearrange("p t w -> p w t"),
                                      axis=AX.X, op=ALU.add)
                    vec.drain()
                vec.engine_nop().then_inc(panel_ready, 1)

            def stats(p, par):
                link = Links(dve, stats_links, 3, p)
                dve.wait_ge(ysum_done, p + 1)
                link(vec.tensor_copy(ysum[:, :], st[:, :]))
                link(vec.scalar_tensor_tensor(out=part[:, :], in0=ysum[:, :], scalar=0.0, in1=ysum[:, :],
                                              op0=ALU.is_le, op1=ALU.add))
                link(vec.scalar_tensor_tensor(out=thr[:, :], in0=thr[:, :], scalar=EPS / THRESH, in1=part[:, :],
                                              op0=ALU.mult, op1=ALU.add))
                rows = slice(32 * par, 32 * par + 1)
                vec.tensor_copy(lrow1[rows, :], part[rows, :]).then_inc(ysum_read, 1)
                dve.wait_ge(ysum_read, p + 1)

            def invert(p, par):
                link = Links(dve, q_links, 1, p)
                link(vec.reciprocal(q[:, :], thr[:, :]))
                rows = slice(32 * par, 32 * par + 1)
                vec.tensor_tensor(out=lrow1[rows, :], in0=lrow1[rows, :], in1=q[rows, :], op=ALU.mult)\
                   .then_inc(q_ready, 1)
                dve.wait_ge(q_ready, p + 1)

            def read_cols(p):
                dve.wait_ge(cols_done, p + 1)
                vec.tensor_copy(q_col[:, bass.ds(p * B, B)], sm[:, 0:B]).then_inc(cols_read, 1)
                vec.tensor_scalar(out=no_edge[:, bass.ds(p * B, B)], in0=sm[:, B:2 * B], scalar1=0.0, scalar2=None,
                                  op0=ALU.is_le).then_inc(cols_read, 1)

            def evacuate1(p, par):
                link = Links(dve, evac1_links, 2, p)
                dve.wait_ge(main1, p * GROUPS + GROUPS)
                dve.wait_ge(xT_in, 16 * (p + 1))
                link(vec.scalar_tensor_tensor(out=xs[:, :], in0=ysum[:, :], scalar=0.0, in1=xT[:, :],
                                              op0=ALU.is_le, op1=ALU.mult))
                link(vec.tensor_tensor(out=xs[:, :], in0=xp[:, par, :], in1=xs[:, :], op=ALU.add))
                vec.tensor_tensor(out=xs[:, :], in0=xs[:, :], in1=q[:, :], op=ALU.mult).then_inc(evac1, 1)
                dve.wait_ge(evac1, p + 1)

            def row_stats(link, rows, blocks, into, done):
                for b in blocks:
                    last = vec.bn_stats(bns[:, b, :], rows(b))
                link(last)
                carry_wait()
                for b in blocks:
                    last = vec.bn_aggr(into[:, b, :], bns[:, b, :])
                last.then_inc(done, 1)

            def normalize1(p, j):
                dve.wait_ge(rstd1, p * 2 + j + 1)
                for b in (2 * j, 2 * j + 1):
                    last = vec.tensor_scalar(out=zn[:, b % 2, :], in0=z_of(b), scalar1=mv[:, b, 0:1],
                                             scalar2=rstd[:, b:b + 1], op0=ALU.subtract, op1=ALU.mult)
                last.then_inc(zn_ready, 1)

            def keep_tc(p, j):
                dve.wait_ge(tc_psum, p * 2 + j + 1)
                vec.tensor_tensor(out=tc[:, bass.ds(p * B + 2 * j, 2), :],
                                  in0=big[:, 3, :].rearrange("p (b d) -> p b d", b=2),
                                  in1=bias2[:, :].unsqueeze(1).to_broadcast([128, 2, 2 * D]), op=ALU.add)\
                   .then_inc(tc_ready, 1)

            def norm1(p):
                link = Links(dve, ln1_links, 2, p)
                for j in range(2):
                    dve.wait_ge(z_done, p * 2 + j + 1)
                    row_stats(link, z_of, (2 * j, 2 * j + 1), mv, ln1_stats)
                normalize1(p, 0)

            def second_half1(p):
                dve.wait_ge(hT_done, p * 2 + 1)
                normalize1(p, 1)
                keep_tc(p, 0)

            def layer1_step(p, par, loads, post, check, ahead):
                if post:
                    evacuate1(p - 1, 1 - par)
                stats(p, par)
                if check:
                    for g in (2, 3):
                        group_sum(p + 1, 1 - par, g, loads[1])
                if post:
                    norm1(p - 1)
                invert(p, par)
                if check:
                    thresholds(p + 1)
                if ahead:
                    group_sum(p + 2, par, 0, loads[2])
                if check:
                    compare(p + 1, 1 - par)
                if post:
                    second_half1(p - 1)
                read_cols(p)
                if check:
                    mask(p + 1, 1 - par)
                if ahead:
                    group_sum(p + 2, par, 1, loads[2])
                if post:
                    keep_tc(p - 1, 1)

            for g in range(GROUPS):
                group_sum(0, 0, g, 1)
            setup()
            thresholds(0)
            compare(0, 0)
            mask(0, 0)
            for g in (0, 1):
                group_sum(1, 1, g, 1)
            layer1_panels(dve, layer1_step)

            def self_loops(p):
                for b in range(B):
                    last = vec.tensor_scalar(out=loop_d[:, b, :], in0=ident[:, :],
                                             scalar1=no_edge[:, bass.ds(p * B + b, 1)], scalar2=None, op0=ALU.mult)
                last.then_inc(loops_ready, 1)

            def spread(row):
                return row[:, :].unsqueeze(1).to_broadcast([128, B, D])

            def finish2(p):
                here = bass.ds(p * B, B)
                link = Links(dve, ln2_links, 7, p)
                dve.wait_ge(z2_done, p + 1)
                for b in range(B):
                    last = vec.scalar_tensor_tensor(out=r[:, b, :], in0=st4[:, b, :],
                                                    scalar=q_col[:, bass.ds(p * B + b, 1)],
                                                    in1=tc[:, bass.ds(p * B + b, 1), D:2 * D]
                                                    .rearrange("p a d -> p (a d)"),
                                                    op0=ALU.mult, op1=ALU.add)
                link(last)
                row_stats(link, lambda b: r[:, b, :], range(B), mv2, ln2_stats)
                dve.wait_ge(rstd2_ready, p * 3 + 1)
                for b in range(B):
                    last = vec.tensor_scalar(out=r[:, b, :], in0=r[:, b, :], scalar1=mv2[:, b, 0:1],
                                             scalar2=rstd2[:, 0, b:b + 1], op0=ALU.subtract, op1=ALU.mult)
                link(last)
                link(vec.tensor_tensor(out=r[:, :, :], in0=r[:, :, :], in1=spread(gamma2), op=ALU.mult))
                link(vec.tensor_tensor(out=r[:, :, :], in0=r[:, :, :], in1=spread(beta2), op=ALU.add))
                link(vec.scalar_tensor_tensor(out=r[:, :, :], in0=r[:, :, :], scalar=0.0, in1=x[:, here, :],
                                              op0=ALU.max, op1=ALU.add))
                row_stats(link, lambda b: r[:, b, :], range(B), mv2, ln2_stats)
                dve.wait_ge(rstd2_ready, p * 3 + 3)
                for b in range(B):
                    vec.tensor_scalar(out=r2[:, b, :], in0=r[:, b, :], scalar1=mv2[:, b, 0:1],
                                      scalar2=rstd2[:, 1, b:b + 1], op0=ALU.subtract, op1=ALU.mult)
                for b in range(B):
                    last = vec.tensor_scalar(out=x[:, bass.ds(p * B + b, 1), :].rearrange("p a d -> p (a d)"),
                                             in0=r[:, b, :], scalar1=mv2[:, b, 0:1],
                                             scalar2=rstd2[:, 0, b:b + 1], op0=ALU.subtract, op1=ALU.mult)
                last.then_inc(u_ready, 1)
                dve.wait_ge(uTh_ready, p + 1)
                cols = bass.ds(p * W, W)
                vec.tensor_tensor(out=uTl[:, cols], in0=sm[:, :], in1=uTh[:, cols].bitcast(F32), op=ALU.subtract)\
                   .then_inc(uTl_ready, 1)

            evacuate1(P - 1, 1)
            norm1(P - 1)
            second_half1(P - 1)
            keep_tc(P - 1, 1)
            dve.wait_ge(cols_read, 2 * P)
            self_loops(0)
            dve.wait_ge(consts2_in, 16 * len(CONSTS2))

            def layer2_step(p, par):
                dve.wait_ge(main2, p * GROUPS)
                self_loops(p)
                finish2(p - 1)

            panels(dve, layer2_step)
            layer2_step(P - 1, 1)

            def finish3(p, piece):
                here = bass.ds(p * B, B)
                link = Links(dve, ln3_links, 4, p, before=(0, 2, 3, 4)[piece])
                if piece == 0:
                    link(vec.tensor_tensor(out=r[:, :, :], in0=x[:, here, :], in1=spread(bias3), op=ALU.add))
                    dve.wait_ge(z3_done, p + 1)
                    link(vec.reciprocal(rden[:, :], sm[:, 0:B]))
                if piece == 1:
                    for b in range(B):
                        last = vec.scalar_tensor_tensor(out=r[:, b, :], in0=st4[:, b, :], scalar=rden[:, b:b + 1],
                                                        in1=r[:, b, :], op0=ALU.mult, op1=ALU.add)
                    link(last)
                if piece == 2:
                    row_stats(link, lambda b: r[:, b, :], range(B), mv2, ln3_stats)
                if piece == 3:
                    dve.wait_ge(rstd3, p + 1)
                    if not (isinstance(p, int) and p == 0):
                        dve.wait_ge(out_stored, 16 * p)
                    for b in range(B):
                        last = vec.tensor_scalar(out=r2[:, b, :], in0=r[:, b, :], scalar1=mv2[:, b, 0:1],
                                                 scalar2=rstd2[:, 0, b:b + 1], op0=ALU.subtract, op1=ALU.mult)
                    last.then_inc(out_ready, 1)
                    dve.wait_ge(out_ready, p + 1)

            def split_x(g):
                tiles = slice(2 * g, 2 * g + 2)
                vec.tensor_copy(xh[:, tiles, 0:D - 1], x[:, tiles, 0:D - 1]).then_inc(xh_ready, 1)
                dve.wait_ge(xh_ready, g + 1)
                vec.tensor_tensor(out=xl[:, tiles, 0:D - 1], in0=x[:, tiles, 0:D - 1],
                                  in1=xh[:, tiles, 0:D - 1].bitcast(F32), op=ALU.subtract).then_inc(xl_ready, 1)

            def weights_low(p, g):
                if g in HIGH_ON_DVE:
                    if not (isinstance(p, int) and p == 0 and g < 4):
                        dve.wait_ge(pv_done, p * PAIRS + g - 3)
                    n = HIGH_ON_DVE.index(g)
                    vec.tensor_copy(ph[:, g % 4, :], pw[:, g % 2, :]).then_inc(ph_dve, 1)
                    dve.wait_ge(ph_dve, p * len(HIGH_ON_DVE) + n + 1)
                else:
                    n = len([k for k in range(g + 1) if k not in HIGH_ON_DVE])
                    dve.wait_ge(ph_ready, p * (PAIRS - len(HIGH_ON_DVE)) + n)
                vec.tensor_tensor(out=pl[:, g % 4, :], in0=pw[:, g % 2, :], in1=ph[:, g % 4, :].bitcast(F32),
                                  op=ALU.subtract).then_inc(pl_ready, 1)

            def layer3_step(p, par, post, first=False):
                for g in range(PAIRS):
                    if FINISH_AT <= g < FINISH_AT + 4 and post is not None:
                        finish3(post, g - FINISH_AT)
                    if first:
                        split_x(g)
                    slot = g // (TG // 2)
                    if g % (TG // 2) == 0:
                        dve.wait_ge(slot_in[0][slot], (p + (P // 2 + P + 1)) * 16)
                    dve.wait_ge(exp_done, p * PAIRS + g + 1)
                    if not (first and g < 2):
                        dve.wait_ge(pl_ready, p * PAIRS + g - 1)
                    vec.tensor_tensor(out=pw[:, g % 2, :], in0=e[:, g % 2, :],
                                      in1=adjA[:, 2 * g:2 * g + 2, :].rearrange("p a w -> p (a w)"), op=ALU.mult)\
                       .then_inc(w_ready, 1)
                    if g in HIGH_ON_DVE:
                        dve.wait_ge(w_ready, p * PAIRS + g + 1)
                    if g > 0:
                        weights_low(p, g - 1)
                    elif not first:
                        weights_low(p - 1, PAIRS - 1)

            finish2(P - 1)
            vec.tensor_tensor(out=w3[:, :], in0=w3[:, :], in1=w3_last[:, :], op=ALU.subtract).then_inc(w3_ready, 1)
            dve.wait_ge(u_ready, P)
            vec.tensor_copy(xh[:, :, D - 1], ones[:, 0:NB]).then_inc(x_last_ready, 1)
            vec.tensor_scalar(out=xl[:, :, D - 1], in0=ones[:, 0:NB], scalar1=0.0, scalar2=None, op0=ALU.mult)\
               .then_inc(x_last_ready, 1)
            layer3_step(0, 0, None, first=True)
            layer3_step(1, 1, 0)
            with dve.Fori(0, LOOPS) as i:
                layer3_step(i * 2 + 2, 0, i * 2 + 1)
                layer3_step(i * 2 + 3, 1, i * 2 + 2)
            weights_low(P - 1, PAIRS - 1)
            for piece in range(4):
                finish3(P - 1, piece)

        @block.tensor
        def _(pe):
            mm = nc.tensor.matmul
            pe.wait_ge(pool_consts, 6)
            pe.wait_ge(consts_in, 16 * N_CONSTS)
            for h in range(2):
                mm(big[:, 0, 0:H], w_in1T[:, h, :], w_out1[:, h, :], start=h == 0, stop=h == 1)
            for h in range(2):
                last = mm(big[0:1, 1, 0:H], b_in1[:, h:h + 1], w_out1[:, h, :], start=h == 0, stop=h == 1)
            last.then_inc(setup_mm, 1)

            def column_sums(p, par):
                pe.wait_ge(sums_links, (2 * GROUPS - 1) * (p + 1))
                mm(st[:, :], ones[:, :], sums[:, par, :], start=True, stop=True).then_inc(csum_done, 1)

            def count(p):
                pe.wait_ge(diff_ready, p + 1)
                mm(sm[0:1, 8:9], cdiff[:, :], ones[:, 0:1], start=True, stop=True).then_inc(count_done, 1)

            def z_products(p, par):
                rows = slice(32 * par, 32 * par + 3)
                pe.wait_ge(evac1, p + 1)
                for b in range(B):
                    cols = slice(b * 128, (b + 1) * 128)
                    mm(z_of(b), xs[:, cols], v1[:, :], start=True, stop=False)
                    mm(z_of(b), xT[:, cols], w_self1[:, :], start=False, stop=False)
                    last = mm(z_of(b), lrow1[rows, cols], brow1[rows, :], start=False, stop=True)
                    if b % 2:
                        last.then_inc(z_done, 1)

            def transposes(p, j):
                pe.wait_ge(zn_ready, p * 2 + j + 1)
                for b in range(2):
                    for h in range(2):
                        last = nc.tensor.transpose(big[:, 2, h * 256 + b * 128:h * 256 + (b + 1) * 128],
                                                   zn[:, b, h * 128:(h + 1) * 128], ident[:, :])
                last.then_inc(hT_done, 1)

            def tc_products(p, j):
                pe.wait_ge(h1T_ready, p * 2 + j + 1)
                if j:
                    pe.wait_ge(tc_ready, p * 2 + 1)
                for b in range(2):
                    for h in range(2):
                        last = mm(big[:, 3, b * 256:(b + 1) * 256], h1T[:, h, b, :], w_cat2[:, h, :],
                                  start=h == 0, stop=h == 1)
                last.then_inc(tc_psum, 1)

            def columns(p):
                pe.wait_ge(q_ready, p + 1)
                for i, row in enumerate((q, ysum)):
                    for b in range(B):
                        last = mm(sm[:, i * B + b:i * B + b + 1], row[0:1, b * 128:(b + 1) * 128], ones[0:1, 0:1],
                                  start=True, stop=True)
                last.then_inc(cols_done, 1)

            def main(par, src, lhs, g, done, part=slice(0, TG)):
                for k in range(g * TG, (g + 1) * TG)[part]:
                    last = mm(xp[:, par, :], lhs(k), src[:, k, :], start=k == 0, stop=k == TILES - 1)
                if part.stop == TG:
                    last.then_inc(done, 1)

            def layer1_step(p, par, loads, post, check, ahead):
                def main1_group(g, part=slice(0, TG)):
                    main(par, adj_of[par], lambda k: x[:, k, :], g, main1, part)

                pe.wait_ge(panel_ready, p + 1)
                mm(st[:, :], ones[:, :], sums[:, par, :], start=True, stop=True).then_inc(ysum_done, 1)
                main1_group(0)
                if post:
                    z_products(p - 1, 1 - par)
                main1_group(1)
                if check:
                    pe.wait_ge(ysum_read, p + 1)
                    column_sums(p + 1, 1 - par)
                if post:
                    transposes(p - 1, 0)
                main1_group(2)
                if post:
                    tc_products(p - 1, 0)
                columns(p)
                main1_group(3, slice(0, TG // 2))
                if post:
                    transposes(p - 1, 1)
                if check:
                    pe.wait_ge(cols_read, 2 * p + 2)
                    count(p + 1)
                main1_group(3, slice(TG // 2, TG))
                if post:
                    tc_products(p - 1, 1)
                else:
                    pe.wait_ge(brow_copied, 16)

            column_sums(0, 0)
            count(0)
            pe.wait_ge(x_in, 16)
            layer1_panels(pe, layer1_step)

            def main2_group(p, par, g):
                pe.wait_ge(slot_in[0][g], (p + (P // 2 + 1)) * 16)
                if g == GROUPS - 1:
                    pe.wait_ge(t2s_ready, p + 1)
                    pe.wait_ge(loops_ready, p + 1)
                    for b in range(B):
                        mm(xp[:, par, b * 128:(b + 1) * 128], t2s[:, b, :], loop_d[:, b, :], start=False, stop=False)
                main(par, adjA, lambda k: tc[:, k, 0:D], g, main2)

            def z2_products(p):
                pe.wait_ge(evac2, p + 1)
                for b in range(B):
                    last = mm(st4[:, b, :], xs2[:, b * 128:(b + 1) * 128], w_out2[:, :], start=True, stop=True)
                last.then_inc(z2_done, 1)

            def u_transposes(p):
                pe.wait_ge(u_ready, p + 1)
                for b in range(B):
                    last = nc.tensor.transpose(sm[:, b * 128:(b + 1) * 128], r2[:, b, :], ident[:, :])
                last.then_inc(uT_done, 1)

            def rows_known(g):
                pe.wait_ge(tc_ready, 2 * (((g + 1) * TG + B - 1) // B))

            rows_known(0)
            main2_group(0, 0, 0)
            z_products(P - 1, 1)
            if GROUPS * B < TILES:
                rows_known(1)
                main2_group(0, 0, 1)
            transposes(P - 1, 0)
            if GROUPS * B < TILES:
                rows_known(2)
                main2_group(0, 0, 2)
            tc_products(P - 1, 0)
            transposes(P - 1, 1)
            tc_products(P - 1, 1)
            for g in (range(3, 4) if GROUPS * B < TILES else range(1, 4)):
                rows_known(g)
                main2_group(0, 0, g)
            pe.wait_ge(consts2_in, 16 * len(CONSTS2))

            def layer2_step(p, par):
                main2_group(p, par, 0)
                z2_products(p - 1)
                main2_group(p, par, 1)
                main2_group(p, par, 2)
                u_transposes(p - 1)
                main2_group(p, par, 3)

            panels(pe, layer2_step)
            layer2_step(P - 1, 1)

            def scores(p, g, first):
                if first:
                    pe.wait_ge(uTl_ready, (2 * g + 1) // B + 1)
                if not (first and g < 2):
                    pe.wait_ge(exp_done, p * PAIRS + g - 1)
                cols = bass.ds(p * W, W)
                for k in range(2):
                    tile = slice((2 * g + k) * 128, (2 * g + k + 1) * 128)
                    s = big[:, 2 * (g % 2) + k, :]
                    mm(s, uTh[:, tile], uTh[:, cols], start=True, stop=False)
                    mm(s, uTh[:, tile], uTl[:, cols], start=False, stop=False)
                    last = mm(s, uTl[:, tile], uTh[:, cols], start=False, stop=True)
                last.then_inc(s_done, 1)

            def weighted(p, par, g, first=False):
                pe.wait_ge(pl_ready, p * PAIRS + g + 1)
                if first:
                    pe.wait_ge(xl_ready, g + 1)
                for k in range(2):
                    cols = slice(k * W, (k + 1) * W)
                    tile = 2 * g + k
                    mm(xp[:, par, :], xh[:, tile, :], ph[:, g % 4, cols], start=g == 0 and k == 0, stop=False)
                    mm(xp[:, par, :], xl[:, tile, :], ph[:, g % 4, cols], start=False, stop=False)
                    last = mm(xp[:, par, :], xh[:, tile, :], pl[:, g % 4, cols], start=False,
                              stop=g == PAIRS - 1 and k == 1)
                last.then_inc(pv_done, 1)

            def z3_products(p, par):
                pe.wait_ge(evac3, p + 1)
                for b in range(B):
                    cols = slice(b * 128, (b + 1) * 128)
                    mm(st4[:, b, :], xs2[:, cols], w3[:, :], start=True, stop=True)
                    last = mm(sm[:, b:b + 1], xs2[:, cols], ident[:, D - 1:D], start=True, stop=True)
                last.then_inc(z3_done, 1)

            def layer3_step(p, par, first=False):
                for g in range(PAIRS):
                    if first and g == 0:
                        z2_products(P - 1)
                    if first and g == 2:
                        u_transposes(P - 1)
                    scores(p, g, first)
                    if g >= LAG:
                        weighted(p, par, g - LAG, first)
                    elif not first:
                        weighted(p - 1, 1 - par, PAIRS - LAG + g)
                    if g == Z3_AT and not first:
                        z3_products(p - 1, 1 - par)

            layer3_step(0, 0, first=True)
            pe.wait_ge(w3_ready, 1)
            panels(pe, layer3_step)
            layer3_step(P - 1, 1)
            for g in range(PAIRS - LAG, PAIRS):
                weighted(P - 1, 1, g)
            z3_products(P - 1, 1)


Z3_AT = 5
FINISH_AT = 6
LAG = 3
HIGH_ON_DVE = (2, 14)


def run_kernel_program(nc, tensors):
    build_program(nc, tensors)


def layouts(i):
    import numpy as np

    def blocks(a):
        return a.reshape(-1, 128, a.shape[1]).transpose(1, 0, 2)

    def panels_of(a):
        n = a.shape[0]
        return a.reshape(n // 128, 128, n // W, W).transpose(2, 1, 0, 3)

    def over_partitions(a):
        return np.broadcast_to(a.reshape(1, -1), (128, a.size))

    x, adj = i["x"], i["adj"]
    n = x.shape[0]
    out = {
        "x": blocks(x),
        "xT": x.T.reshape(x.shape[1], n // W, W).transpose(1, 0, 2),
        "adj": panels_of(adj),
        "adjT": panels_of(adj.T),
        "w_in1T": blocks(i["L0_gnn_W_in1"].T),
        "w_out1": blocks(i["L0_gnn_W_out1"]),
        "w_self1": i["L0_gnn_W_self1"],
        "b_in1": i["L0_gnn_b_in1"].reshape(2, 128).T,
        "b_out1": i["L0_gnn_b_out1"].reshape(1, -1),
        "b_self1": i["L0_gnn_b_self1"].reshape(1, -1),
        "g1": i["L0_gnn_g1"].reshape(2, 128).T,
        "be1": i["L0_gnn_be1"].reshape(2, 128).T,
        "w_cat2": blocks(np.concatenate([i["L0_gnn_W_in2"], i["L0_gnn_W_self2"]], axis=1)),
        "b_in2": over_partitions(i["L0_gnn_b_in2"]),
        "b_out2": over_partitions(i["L0_gnn_b_out2"]),
        "b_self2": over_partitions(i["L0_gnn_b_self2"]),
        "w_out2": i["L0_gnn_W_out2"],
        "g2": over_partitions(i["L0_gnn_g2"]),
        "be2": over_partitions(i["L0_gnn_be2"]),
        "w3T": i["L1_gnn_W"].T,
        "w3T_last": over_partitions(i["L1_gnn_W"][:, -1]),
        "bias3": over_partitions(i["L1_gnn_bias"]),
        "b": over_partitions(i["L1_gnn_b"]),
    }
    return {k: np.ascontiguousarray(v) for k, v in out.items()}


def kernel(**inputs):
    import numpy as np
    import concourse.bacc as bacc
    from concourse.bass_utils import run_bass_kernel_spmd

    arrays = layouts({k: np.asarray(v) for k, v in inputs.items()})
    n, d = np.asarray(inputs["x"]).shape
    nc = bacc.Bacc("TRN2", target_bir_lowering=False, num_devices=1)
    tensors = {k: nc.dram_tensor(f"in_{k}", a.shape, mybir.dt.from_np(a.dtype), kind="ExternalInput").ap()
               for k, a in arrays.items()}
    tensors["out"] = nc.dram_tensor("out_rows", (n // W, 128, B, d), F32, kind="ExternalOutput").ap()
    build_program(nc, tensors)
    result = run_bass_kernel_spmd(nc, [{f"in_{k}": a for k, a in arrays.items()}], core_ids=[0])
    rows = result.results[0]["out_rows"]
    return rows.transpose(0, 2, 1, 3).reshape(n, d)
```

```python
from contextlib import ExitStack

import concourse.bass as bass
from concourse import mybir

F32 = mybir.dt.float32
F32R = mybir.dt.float32r
I8 = mybir.dt.int8
I32 = mybir.dt.int32
ALU = mybir.AluOpType
ACT = mybir.ActivationFunctionType
AX = mybir.AxisListType

THRESH = 1e-6
EPS = 1e-8
LN_EPS = 1e-5
TANH_RANGE = 8.0

W = 512
B = W // 128
GROUPS = 4
SBUF_START = 16512
SBUF_END = 229344
KIB = 1024


class Links:

    def __init__(self, eng, sem, count, panel, before=0):
        self.eng, self.sem, self.first, self.n = eng, sem, panel * count, before

    def __call__(self, ins):
        ins.then_inc(self.sem, 1)
        self.n += 1
        self.eng.wait_ge(self.sem, self.first + self.n)


def build_program(nc, t):
    NB = t["x"].shape[1]
    TILES = NB
    N = NB * 128
    P = N // W
    TG = TILES // GROUPS
    PAIRS = TILES // 2
    LOOPS = (P - 2) // 2
    D, H = 128, 256
    SPLIT2 = [k for k in range(TILES) if k % 2]
    S2 = len(SPLIT2)
    SG = S2 // GROUPS
    RING2 = 4
    SPLIT = [g for g in range(PAIRS) if g % WHOLE_EVERY != WHOLE_EVERY - 1]
    WHOLE = [g for g in range(PAIRS) if g not in SPLIT]
    S = len(SPLIT)
    HIGH_ON_ACT = [g for g in SPLIT if g not in HIGH_ON_DVE]
    HALF = TG * W // 2
    BOUND = 1.001 * THRESH * N

    ctx = ExitStack()
    with ctx:
        place = [SBUF_START]

        def at(name, shape, dt=F32, offset=None):
            size = 1 if dt == I8 else 4
            for s in shape[1:]:
                size *= s
            if offset is None:
                offset = place[0]
                place[0] += (size + 31) // 32 * 32
            return nc.alloc_sbuf_tensor_at(name, shape, dt, offset=offset)

        def sem(name):
            return ctx.enter_context(nc.semaphore(name))

        adjA = at("adjA", [128, TILES, W])
        b_start = place[0]
        adjB = at("adjB", [128, TILES, W])
        b_end = place[0] = b_start + 64 * KIB
        adj_of = (adjA, adjB)
        x = at("x_nodes", [128, NB, D])
        tc_start = place[0]
        tc = at("t2_self2", [128, NB, 2 * D])
        tc_end = place[0]
        ident = at("ident", [128, 128])
        ones = at("ones", [128, 128])
        layer1_start = place[0]
        xT = at("xT_panel", [128, W])
        w_self1 = at("w_self1_sb", [128, H])
        w_cat2 = at("w_in2_self2", [128, 2, 2 * D])
        v1 = at("w_in1_w_out1", [128, H])
        brow1 = at("bias_rows1", [35, H])
        lrow1 = at("bias_left1", [35, W])
        bias2 = at("bias2", [128, 2 * D])
        sums = at("column_sums", [128, 2, W])
        part = at("part_sums", [128, W])
        thr = at("thresholds", [128, W])
        ysum = at("edge_sums", [128, W])
        q = at("q_row", [128, W])
        xs = at("scaled_x", [128, W])
        zn = at("z_normed", [128, 2, H])
        h1T = at("h1T", [128, 2, 2, 128])
        junk_start = place[0]
        junk = at("sign_out", [128, 2048], I8)
        layer1_end = place[0]
        g1c = at("gamma1", [128, 2])
        be1c = at("beta1", [128, 2])
        q_col = at("q_col", [128, NB])
        no_edge = at("no_edge", [128, NB])
        minus_half = at("minus_half", [128, B])
        eps_row = at("eps_row", [128, B])
        width_row = at("width_row", [128, B])
        counts = at("sign_counts", [128, 2, 2, 2 * GROUPS])
        flags = at("flags", [1, P], I32)
        bns = at("bn_stats_out", [128, B, 6])
        mv = at("mean_var", [128, B, 2])
        vtmp = at("var_tmp", [128, B])
        rstd = at("rstd", [128, B])
        scalars = at("scalars", [128, 5])
        cmax, cdiff, minus_bound, b_eighth, pool_idle = (scalars[:, i:i + 1] for i in range(5))
        pool_idle = pool_idle[0:1, :]
        idle = at("idle", [1, 1])
        assert place[0] <= SBUF_END, place[0]
        w_in1T = at("w_in1T_sb", [128, 2, D], offset=tc_start)
        w_out1 = at("w_out1_sb", [128, 2, H], offset=tc_start + KIB)
        b_in1 = at("b_in1_sb", [128, 2], offset=tc_start + 3 * KIB)
        b_self2 = at("b_self2_sb", [128, D], offset=tc_start + 4 * KIB)
        place[0] = b_start
        uTh = at("uT_high", [128, N], F32R)
        uTl = at("uT_low", [128, N], F32R)
        w3 = at("w3T_sb", [128, D])
        w3_last = at("w3T_last_row", [128, D])
        bias3 = at("bias3_sb", [128, D])
        xs2 = at("x_out", [128, W])
        r = at("rows", [128, B, D])
        r2 = at("rows_out", [128, B, D])
        mv2 = at("mean_var2", [128, B, 2])
        vtmp2 = at("var_tmp2", [128, 2, B])
        rstd2 = at("rstd2", [128, 2, B])
        rden = at("inv_weight_sum", [128, B])
        layer2_start = place[0]
        loop_d = at("self_loops", [128, B, 128])
        t2s = at("t2_blocks", [128, B, D])
        ah = at("adj_high", [128, RING2, W], F32R)
        al = at("adj_low", [128, RING2, W], F32R)
        thr2 = at("thresholds2", [128, W])
        above = at("above_threshold", [128, W])
        assert place[0] <= b_end, (place[0], b_end)
        place[0] = layer1_start
        th = at("t2_high", [128, S2, D], F32R)
        tl = at("t2_low", [128, S2, D], F32R)
        assert place[0] <= junk_start
        above_first = at("above_threshold_first", [128, W], offset=junk_start)
        place[0] = junk_start
        w_out2 = at("w_out2_sb", [128, D])
        gamma2 = at("gamma2", [128, D])
        beta2 = at("beta2", [128, D])
        assert place[0] <= layer1_end, (place[0], layer1_end)
        place[0] = layer2_start
        pw = at("weights3", [128, 2, 2 * W])
        ph = at("weights3_high", [128, 4, 2 * W], F32R)
        assert place[0] <= b_end, (place[0], b_end)
        place[0] = layer1_start
        pl = at("weights3_low", [128, 4, 2 * W], F32R)
        e = at("exp_out", [128, 2, 2 * W])
        pn = at("weights3_whole", [128, 2 * W])
        assert place[0] <= junk_start, (place[0], junk_start)
        place[0] = tc_start
        xh = at("x_high", [128, 2 * S, D], F32R)
        xl = at("x_low", [128, 2 * S, D], F32R)
        xo = at("x_with_ones", [128, 2 * len(WHOLE), D])
        assert place[0] <= tc_end

        xp = ctx.enter_context(nc.psum_tensor("xp", [128, 2, W], F32))
        st = ctx.enter_context(nc.psum_tensor("st", [128, W], F32))
        sm = ctx.enter_context(nc.psum_tensor("sm", [128, W], F32))
        big = ctx.enter_context(nc.psum_tensor("big", [128, 4, W], F32))
        st4 = st[:, :].rearrange("p (b d) -> p b d", b=B)

        def z_of(b):
            return big[:, b // 2, (b % 2) * H:(b % 2 + 1) * H]

        slot_in = [[sem(f"slot_in{i}{g}") for g in range(GROUPS)] for i in range(2)]
        x_in = sem("x_in")
        xT_in = sem("xT_in")
        consts_in = sem("consts_in")
        consts2_in = sem("consts2_in")
        brow_copied = sem("brow_copied")
        ident_zero = sem("ident_zero")
        pool_consts = sem("pool_consts")
        dve_consts = sem("dve_consts")
        setup_mm = sem("setup_mm")
        weights_ready = sem("weights_ready")
        sums_links = sem("sums_links")
        csum_done = sem("csum_done")
        thr_ready = sem("thr_ready")
        thr_saved = sem("thr_saved")
        thr2_in = sem("thr2_in")
        group_masked = sem("group_masked")
        mask2_links = sem("mask2_links")
        signs_done = sem("signs_done")
        diff_links = sem("diff_links")
        flag_links = sem("flag_links")
        diff_ready = sem("diff_ready")
        count_done = sem("count_done")
        panel_ready = sem("panel_ready")
        ysum_done = sem("ysum_done")
        stats_links = sem("stats_links")
        ysum_read = sem("ysum_read")
        q_links = sem("q_links")
        q_ready = sem("q_ready")
        cols_done = sem("cols_done")
        cols_read = sem("cols_read")
        main1 = sem("main1_group")
        evac1_links = sem("evac1_links")
        evac1 = sem("evac1_done")
        z_done = sem("z_done")
        ln1_links = sem("ln1_links")
        ln1_stats = sem("ln1_stats")
        pool1_links = sem("pool1_links")
        rstd1 = sem("rstd1_ready")
        zn_ready = sem("zn_ready")
        hT_done = sem("hT_done")
        h1T_ready = sem("h1T_ready")
        tc_psum = sem("tc_psum_done")
        tc_ready = sem("tc_ready")
        main2 = sem("main2_group")
        loops_ready = sem("loops_ready")
        t2s_ready = sem("t2s_ready")
        th_ready = sem("th_ready")
        tl_ready = sem("tl_ready")
        ah_ready = sem("ah_ready")
        al_ready = sem("al_ready")
        split2_used = sem("split2_used")
        evac2 = sem("evac2_done")
        z2_done = sem("z2_done")
        ln2_links = sem("ln2_links")
        ln2_stats = sem("ln2_stats")
        pool2_links = sem("pool2_links")
        rstd2_ready = sem("rstd2_ready")
        u_ready = sem("u_ready")
        x_ready = sem("x_ready")
        uT_done = sem("uT_psum_done")
        uTh_ready = sem("uTh_ready")
        uTl_ready = sem("uTl_ready")
        s_done = sem("s_done")
        tanh_done = sem("tanh_done")
        exp_done = sem("exp_done")
        w_ready = sem("w_ready")
        ph_ready = sem("ph_ready")
        ph_dve = sem("ph_dve")
        pl_ready = sem("pl_ready")
        w3_ready = sem("w3_ready")
        x_last_ready = sem("x_last_ready")
        xh_ready = sem("xh_ready")
        xl_ready = sem("xl_ready")
        xo_ready = sem("xo_ready")
        pv_done = sem("pv_done")
        evac3 = sem("evac3_done")
        z3_done = sem("z3_done")
        ln3_links = sem("ln3_links")
        ln3_stats = sem("ln3_stats")
        pool3_links = sem("pool3_links")
        rstd3 = sem("rstd3_ready")
        out_ready = sem("out_ready")
        out_stored = sem("out_stored")

        MATRICES = ((w_in1T, "w_in1T"), (w_out1, "w_out1"), (w_cat2, "w_cat2"))
        ROWS = ((b_in1, "b_in1"), (w_self1, "w_self1"), (g1c, "g1"), (be1c, "be1"), (b_self2, "b_self2"),
                (b_eighth, "b"))
        CONSTS2 = ((w_out2, "w_out2"), (w3, "w3T"), (w3_last, "w3T_last"), (gamma2, "g2"), (beta2, "be2"),
                   (bias3, "bias3"))
        N_CONSTS = len(MATRICES) + len(ROWS) + 4

        def split_used(p, n):
            if n < 0:
                p, n = p - 1, n + S2
            g, k = divmod(n, SG)
            if k == SG - 1:
                return main2, p * GROUPS + g + 1
            return split2_used, (p - 1) * (S2 - GROUPS) + g * (SG - 1) + k + 1

        def products_done(p, split_pair):
            if split_pair < 0:
                return (p - 1) * PAIRS + SPLIT[split_pair + S] + 1
            return p * PAIRS + SPLIT[split_pair] + 1

        def panels(eng, step):
            with eng.Fori(0, LOOPS) as i:
                step(i * 2 + 1, 1)
                step(i * 2 + 2, 0)

        def layer1_panels(eng, step):
            def at_panel(p, **has):
                step(p, p % 2, {a: (p + a) // 2 + 1 for a in (1, 2)}, **has)

            at_panel(0, post=False, check=True, ahead=True)
            if LOOPS > 1:
                with eng.Fori(0, LOOPS - 1) as i:
                    for c in (1, 2):
                        step(i * 2 + c, c % 2, {a: i + (c + a) // 2 + 1 for a in (1, 2)},
                             post=True, check=True, ahead=True)
            at_panel(P - 3, post=True, check=True, ahead=True)
            at_panel(P - 2, post=True, check=True, ahead=False)
            at_panel(P - 1, post=True, check=False, ahead=False)

        saved = nc.dram_tensor("saved_thresholds", (P, 1, W), F32, kind="Internal").ap()

        block = ctx.enter_context(nc.Block())

        @block.sync
        def _(sp):
            def load_group(into, src, p, g):
                sp.dma_start(adj_of[into][:, g * TG:(g + 1) * TG, :], src[p, :, g * TG:(g + 1) * TG, :])\
                  .then_inc(slot_in[into][g], 16)

            load_group(0, t["adj"], 0, 0)
            sp.wait_ge(consts_in, 16 * N_CONSTS)
            for g in range(1, GROUPS):
                load_group(0, t["adj"], 0, g)
            sp.dma_start(x[:, :, :], t["x"]).then_inc(x_in, 16)
            sp.dma_start(xT[:, :], t["xT"][0]).then_inc(xT_in, 16)
            for g in range(GROUPS):
                load_group(1, t["adj"], 1, g)
            sp.wait_ge(weights_ready, 2)
            sp.dma_start(brow1[32:35, :], brow1[0:3, :]).then_inc(brow_copied, 16)

            def layer1_loads(p, par):
                for g in range(GROUPS):
                    sp.wait_ge(main1, (p - 1) * GROUPS + g + 1)
                    load_group(1 - par, t["adj"], p + 1, g)
                sp.wait_ge(z_done, p * 2)
                sp.dma_start(xT[:, :], t["xT"][p]).then_inc(xT_in, 16)

            panels(sp, layer1_loads)
            def load_thresholds(into, p):
                sp.dma_start(into, saved[p].to_broadcast([128, W])).then_inc(thr2_in, 16)

            for g in range(GROUPS):
                sp.wait_ge(main1, (P - 2) * GROUPS + g + 1)
                load_group(0, t["adj"], 0, g)
            sp.wait_ge(thr_saved, 16 * P)
            load_thresholds(sums[:, 0, :], 0)
            sp.wait_ge(z_done, (P - 1) * 2)
            sp.dma_start(xT[:, :], t["xT"][P - 1]).then_inc(xT_in, 16)
            sp.wait_ge(main1, P * GROUPS)
            sp.wait_ge(group_masked, GROUPS)
            for dst, name in CONSTS2:
                sp.dma_start(dst[:, :], t[name]).then_inc(consts2_in, 16)

            def layer2_loads(p, par):
                for g in range(GROUPS):
                    sp.wait_ge(main2, (p - 1) * GROUPS + g + 1)
                    load_group(0, t["adj"], p, g)
                    if g == 0:
                        sp.wait_ge(group_masked, p * GROUPS)
                        load_thresholds(thr2[:, :], p)

            panels(sp, layer2_loads)
            layer2_loads(P - 1, 1)
            for g in range(GROUPS):
                sp.wait_ge(main2, (P - 1) * GROUPS + g + 1)
                load_group(0, t["adjT"], 0, g)

            def layer3_loads(p):
                for g in range(GROUPS):
                    sp.wait_ge(w_ready, (p - 1) * PAIRS + (g + 1) * (TG // 2))
                    load_group(0, t["adjT"], p, g)

            def store(p):
                sp.wait_ge(out_ready, p + 1)
                sp.dma_start(t["out"][p], r2[:, :, :]).then_inc(out_stored, 16)

            layer3_loads(1)
            with sp.Fori(0, LOOPS) as i:
                for c in (0, 1):
                    layer3_loads(i * 2 + 2 + c)
                    store(i * 2 + c)
            store(P - 2)
            store(P - 1)
            sp.wait_ge(out_stored, 16 * P)

        @block.gpsimd
        def _(pool):
            gp = nc.gpsimd
            gp.memset(minus_bound[:, :], -BOUND).then_inc(pool_consts, 1)
            gp.memset(ones[:, :], 1.0).then_inc(pool_consts, 1)
            gp.memset(minus_half[:, :], -0.5).then_inc(pool_consts, 1)
            gp.memset(eps_row[:, :], LN_EPS).then_inc(pool_consts, 1)
            gp.memset(width_row[:, :], float(D)).then_inc(pool_consts, 1)
            gp.memset(ident[:, :], 0.0).then_inc(ident_zero, 1)
            pool.wait_ge(ident_zero, 1)
            gp.affine_select(out=ident[:, :], in_=ident[:, :], compare_op=ALU.not_equal, fill=1.0,
                             base=0, pattern=[[-1, 128]], channel_multiplier=1).then_inc(pool_consts, 1)
            pool.wait_ge(pool_consts, 6)

            def powers1(p):
                link = Links(pool, pool1_links, 2, p)
                for j in range(2):
                    v = slice(2 * j, 2 * j + 2)
                    pool.wait_ge(ln1_stats, p * 2 + j + 1)
                    link(gp.tensor_tensor(out=vtmp[:, v], in0=mv[:, v, 1], in1=eps_row[:, v], op=ALU.add))
                    gp.tensor_tensor(out=rstd[:, v], in0=vtmp[:, v], in1=minus_half[:, v], op=ALU.pow)\
                      .then_inc(rstd1, 1)

            def stage_t2(p):
                gp.tensor_copy(t2s[:, :, :], tc[:, bass.ds(p * B, B), 0:D]).then_inc(t2s_ready, 1)

            def mask2(p, g, first=False):
                limits, mask = (sums[:, 0, :], above_first[:, :]) if first else (thr2[:, :], above[:, :])
                pool.wait_ge(slot_in[0][g], (p + (P // 2 + 1)) * 16)
                pool.wait_ge(thr2_in, 16 * (p + 1))
                gp.tensor_tensor(out=pool_idle, in0=eps_row[0:1, 0:1], in1=eps_row[0:1, 0:1], op=ALU.mult)
                gp.drain()
                flagged = gp.value_load(flags[0:1, bass.ds(p, 1)])
                with pool.If(flagged != 0):
                    with pool.Fori(g * TG, (g + 1) * TG) as k:
                        tile = adjA[:, bass.ds(k, 1), :].rearrange("p a w -> p (a w)")
                        gp.tensor_tensor(out=mask, in0=tile, in1=limits, op=ALU.subtract)
                        gp.drain()
                        gp.tensor_scalar(out=mask, in0=mask, scalar1=0.0, scalar2=None, op0=ALU.is_gt)
                        gp.drain()
                        gp.tensor_tensor(out=tile, in0=tile, in1=mask, op=ALU.mult)
                        gp.drain()
                gp.engine_nop().then_inc(group_masked, 1)

            def powers2(p, between=lambda: None):
                link = Links(pool, pool2_links, 3, p)
                pool.wait_ge(ln2_stats, p * 2 + 1)
                link(gp.tensor_tensor(out=vtmp2[:, 0, :], in0=mv2[:, :, 1], in1=eps_row[:, :], op=ALU.add))
                gp.tensor_tensor(out=rstd2[:, 0, :], in0=vtmp2[:, 0, :], in1=minus_half[:, :], op=ALU.pow)\
                  .then_inc(rstd2_ready, 1)
                between()
                pool.wait_ge(ln2_stats, p * 2 + 2)
                link(gp.tensor_tensor(out=vtmp2[:, 0, :], in0=mv2[:, :, 1], in1=eps_row[:, :], op=ALU.add))
                link(gp.tensor_tensor(out=vtmp2[:, 1, :], in0=mv2[:, :, 1], in1=width_row[:, :], op=ALU.mult))
                for i in range(2):
                    gp.tensor_tensor(out=rstd2[:, i, :], in0=vtmp2[:, i, :], in1=minus_half[:, :], op=ALU.pow)\
                      .then_inc(rstd2_ready, 1)

            def powers3(p):
                link = Links(pool, pool3_links, 1, p)
                pool.wait_ge(ln3_stats, p + 1)
                link(gp.tensor_tensor(out=vtmp2[:, 0, :], in0=mv2[:, :, 1], in1=eps_row[:, :], op=ALU.add))
                gp.tensor_tensor(out=rstd2[:, 0, :], in0=vtmp2[:, 0, :], in1=minus_half[:, :], op=ALU.pow)\
                  .then_inc(rstd3, 1)

            panels(pool, lambda p, par: powers1(p - 1))
            powers1(P - 2)
            pool.wait_ge(signs_done, P * (4 * GROUPS))
            for g in range(GROUPS):
                mask2(0, g, first=True)
            pool.wait_ge(main1, P * GROUPS)
            stage_t2(0)
            powers1(P - 1)

            def layer2_step(p, par, ahead=True):
                pool.wait_ge(main2, p * GROUPS)
                stage_t2(p)
                powers2(p - 1, between=lambda: mask2(p, GROUPS - 1))
                if ahead:
                    for g in range(GROUPS - 1):
                        mask2(p + 1, g)

            for g in range(GROUPS - 1):
                mask2(1, g)
            panels(pool, layer2_step)
            layer2_step(P - 1, 1, ahead=False)
            powers2(P - 1)
            panels(pool, lambda p, par: powers3(p - 1))
            powers3(P - 2)
            powers3(P - 1)

        @block.scalar
        def _(act):
            for dst, name in MATRICES:
                act.dma_start(dst[:, :, :], t[name]).then_inc(consts_in, 16)
            for dst, name in ROWS:
                act.dma_start(dst[:, :], t[name]).then_inc(consts_in, 16)
            act.dma_start(bias2[:, 0:D], t["b_in2"]).then_inc(consts_in, 16)
            act.dma_start(bias2[:, D:2 * D], t["b_out2"]).then_inc(consts_in, 16)
            act.dma_start(brow1[1:2, :], t["b_out1"]).then_inc(consts_in, 16)
            act.dma_start(brow1[2:3, :], t["b_self1"]).then_inc(consts_in, 16)

            def signs(p, par, g, load, halves=(0, 1)):
                act.wait_ge(slot_in[par][g], 16 * load)
                src = adj_of[par][:, g * TG:(g + 1) * TG, :].rearrange("p t w -> p (t w)")
                for h in halves:
                    for which, bias in ((0, 0.0), (1, minus_bound[:, 0:1])):
                        n = 4 * g + 2 * h + which
                        if not (isinstance(p, int) and p == n == 0):
                            act.wait_ge(signs_done, p * (4 * GROUPS) + n)
                        nc.scalar.activation(junk[:, 0:HALF], src[:, h * HALF:(h + 1) * HALF], ACT.Sign, bias=bias,
                                             accum_out=counts[:, par, which, 2 * g + h:2 * g + h + 1])\
                          .then_inc(signs_done, 1)

            def relu_hT(p, j):
                act.wait_ge(hT_done, p * 2 + j + 1)
                for h in range(2):
                    last = nc.scalar.activation(h1T[:, h, :, :].rearrange("p b n -> p (b n)"),
                                                big[:, 2, h * 256:(h + 1) * 256], ACT.Relu,
                                                bias=be1c[:, h:h + 1], scale=g1c[:, h:h + 1])
                last.then_inc(h1T_ready, 1)

            def save_thresholds(p):
                act.wait_ge(thr_ready, 2 * p + 2)
                act.dma_start(saved[p], thr[0:1, :]).then_inc(thr_saved, 16)

            def layer1_step(p, par, loads, post, check, ahead):
                if check:
                    for g in (2, 3):
                        signs(p + 1, 1 - par, g, loads[1])
                if ahead:
                    act.wait_ge(diff_ready, p + 1)
                    signs(p + 2, par, 0, loads[2], (0,))
                if post:
                    relu_hT(p - 1, 0)
                if ahead:
                    signs(p + 2, par, 0, loads[2], (1,))
                    signs(p + 2, par, 1, loads[2], (0,))
                if post:
                    relu_hT(p - 1, 1)
                if check:
                    save_thresholds(p + 1)
                if ahead:
                    signs(p + 2, par, 1, loads[2], (1,))

            act.wait_ge(pool_consts, 1)
            for g in range(GROUPS):
                signs(0, 0, g, 1)
            save_thresholds(0)
            for g in (0, 1):
                signs(1, 1, g, 1)
            act.wait_ge(consts_in, 16 * N_CONSTS)
            layer1_panels(act, layer1_step)
            for j in range(2):
                relu_hT(P - 1, j)

            def evacuate2(p, par):
                act.wait_ge(main2, p * GROUPS + GROUPS)
                nc.scalar.copy(xs2[:, :], xp[:, par, :]).then_inc(evac2, 1)

            def split_high(p):
                act.wait_ge(uT_done, p + 1)
                nc.scalar.copy(uTh[:, bass.ds(p * W, W)], sm[:, :]).then_inc(uTh_ready, 1)

            def adj_high(p, n):
                k = SPLIT2[n]
                if n % SG == 0:
                    act.wait_ge(group_masked, p * GROUPS + n // SG + 1)
                if not (isinstance(p, int) and p == 1 and n < RING2):
                    act.wait_ge(*split_used(p, n - RING2))
                nc.scalar.copy(ah[:, n % RING2, :], adjA[:, k, :]).then_inc(ah_ready, 1)

            def layer2_step(p, par):
                for n in range(S2):
                    if n == 1:
                        evacuate2(p - 1, 1 - par)
                    if n == S2 - 1:
                        split_high(p - 1)
                    adj_high(p, n)

            act.wait_ge(main1, P * GROUPS)
            layer2_step(1, 1)
            with act.Fori(0, LOOPS) as i:
                layer2_step(i * 2 + 2, 0)
                layer2_step(i * 2 + 3, 1)
            act.wait_ge(dve_consts, 3)

            def evacuate3(p, par):
                act.wait_ge(pv_done, p * PAIRS + PAIRS)
                nc.scalar.copy(xs2[:, :], xp[:, par, :]).then_inc(evac3, 1)

            def weights_high(p, g):
                n = SPLIT.index(g)
                act.wait_ge(w_ready, p * PAIRS + g + 1)
                if not (isinstance(p, int) and p == 0 and n < 4):
                    act.wait_ge(pv_done, products_done(p, n - 4))
                nc.scalar.copy(ph[:, n % 4, :], pw[:, n % 2, :]).then_inc(ph_ready, 1)

            def layer3_step(p, par, first=False):
                for g in range(PAIRS):
                    if first and g == 0:
                        evacuate2(P - 1, 1)
                    if first and g == LAST_U_AT + 1:
                        split_high(P - 1)
                    if not first and g == 4:
                        evacuate3(p - 1, 1 - par)
                    s = big[:, 2 * (g % 2):2 * (g % 2) + 2, :].rearrange("p a w -> p (a w)")
                    act.wait_ge(s_done, p * PAIRS + g + 1)
                    nc.scalar.activation(s, s, ACT.Tanh, scale=b_eighth[:, 0:1]).then_inc(tanh_done, 1)
                    act.wait_ge(tanh_done, p * PAIRS + g + 1)
                    if not (first and g < 2):
                        act.wait_ge(w_ready, p * PAIRS + g - 1)
                    nc.scalar.activation(e[:, g % 2, :], s, ACT.Exp, scale=TANH_RANGE).then_inc(exp_done, 1)
                    if g - 1 in HIGH_ON_ACT:
                        weights_high(p, g - 1)

            layer3_step(0, 0, first=True)
            panels(act, layer3_step)
            layer3_step(P - 1, 1)
            evacuate3(P - 1, 1)

        @block.vector
        def _(dve):
            vec = nc.vector

            def carry_wait():
                vec.memset(idle[:, :], 0.0)

            vec.memset(lrow1[:, :], 1.0).then_inc(dve_consts, 1)

            def setup():
                dve.wait_ge(consts_in, 16 * N_CONSTS)
                vec.tensor_scalar(out=b_eighth[:, :], in0=b_eighth[:, :], scalar1=1.0 / TANH_RANGE, scalar2=None,
                                  op0=ALU.mult).then_inc(dve_consts, 1)
                vec.tensor_tensor(out=bias2[:, D:2 * D], in0=bias2[:, D:2 * D], in1=b_self2[:, :], op=ALU.add)\
                   .then_inc(dve_consts, 1)
                dve.wait_ge(setup_mm, 1)
                vec.tensor_copy(v1[:, :], big[:, 0, 0:H]).then_inc(weights_ready, 1)
                vec.tensor_copy(brow1[0:1, :], big[0:1, 1, 0:H]).then_inc(weights_ready, 1)
                dve.wait_ge(dve_consts, 3)

            def group_sum(p, par, g, load):
                dve.wait_ge(slot_in[par][g], 16 * load)
                src = adj_of[par][:, g * TG:(g + 1) * TG, :].rearrange("p t w -> p w t")
                link = Links(dve, sums_links, 2 * GROUPS - 1, p, before=max(2 * g - 1, 0))
                if g == 0:
                    link(vec.tensor_reduce(out=sums[:, par, :], in_=src, axis=AX.X, op=ALU.add))
                else:
                    link(vec.tensor_reduce(out=part[:, :], in_=src, axis=AX.X, op=ALU.add))
                    link(vec.tensor_tensor(out=sums[:, par, :], in0=sums[:, par, :], in1=part[:, :], op=ALU.add))

            def thresholds(p):
                dve.wait_ge(csum_done, p + 1)
                if not (isinstance(p, int) and p == 0):
                    dve.wait_ge(thr_saved, 16 * p)
                vec.tensor_reduce(out=cmax[:, :], in_=st[:, :], axis=AX.X, op=ALU.max).then_inc(thr_ready, 1)
                vec.tensor_scalar(out=thr[:, :], in0=st[:, :], scalar1=EPS, scalar2=THRESH, op0=ALU.add,
                                  op1=ALU.mult).then_inc(thr_ready, 1)
                dve.wait_ge(thr_ready, 2 * p + 2)

            def compare(p, par):
                link = Links(dve, diff_links, 3, p)
                dve.wait_ge(signs_done, (p + 1) * (4 * GROUPS))
                d = counts[:, par, 0, :]
                link(vec.scalar_tensor_tensor(out=d, in0=d, scalar=2.0, in1=counts[:, par, 1, :],
                                              op0=ALU.mult, op1=ALU.subtract))
                link(vec.tensor_scalar(out=d, in0=d, scalar1=float(-HALF), scalar2=0.0, op0=ALU.add,
                                       op1=ALU.not_equal))
                link(vec.tensor_reduce(out=cdiff[:, :], in_=d, axis=AX.X, op=ALU.add))
                vec.scalar_tensor_tensor(out=cdiff[:, :], in0=cmax[:, :], scalar=float(N), in1=cdiff[:, :],
                                         op0=ALU.is_gt, op1=ALU.add).then_inc(diff_ready, 1)

            def mask(p, par):
                link = Links(dve, flag_links, 1, p)
                dve.wait_ge(count_done, p + 1)
                flag = flags[0:1, bass.ds(p, 1)]
                link(vec.tensor_scalar(out=flag, in0=sm[0:1, 8:9], scalar1=1.0, scalar2=None, op0=ALU.min))
                carry_wait()
                flagged = vec.value_load(flag)
                tiles = adj_of[par]
                with dve.If(flagged != 0):
                    with dve.Fori(0, TILES) as k:
                        tile = tiles[:, bass.ds(k, 1), :].rearrange("p a w -> p (a w)")
                        vec.tensor_tensor(out=part[:, :], in0=tile, in1=thr[:, :], op=ALU.is_gt)
                        vec.drain()
                        vec.tensor_tensor(out=tile, in0=tile, in1=part[:, :], op=ALU.mult)
                        vec.drain()
                    vec.tensor_reduce(out=sums[:, par, :], in_=tiles[:, :, :].rearrange("p t w -> p w t"),
                                      axis=AX.X, op=ALU.add)
                    vec.drain()
                vec.engine_nop().then_inc(panel_ready, 1)

            def stats(p, par):
                link = Links(dve, stats_links, 3, p)
                dve.wait_ge(ysum_done, p + 1)
                link(vec.tensor_copy(ysum[:, :], st[:, :]))
                link(vec.scalar_tensor_tensor(out=part[:, :], in0=ysum[:, :], scalar=0.0, in1=ysum[:, :],
                                              op0=ALU.is_le, op1=ALU.add))
                link(vec.scalar_tensor_tensor(out=q[:, :], in0=thr[:, :], scalar=EPS / THRESH, in1=part[:, :],
                                              op0=ALU.mult, op1=ALU.add))
                rows = slice(32 * par, 32 * par + 1)
                vec.tensor_copy(lrow1[rows, :], part[rows, :]).then_inc(ysum_read, 1)
                dve.wait_ge(ysum_read, p + 1)

            def invert(p, par):
                link = Links(dve, q_links, 1, p)
                link(vec.reciprocal(q[:, :], q[:, :]))
                rows = slice(32 * par, 32 * par + 1)
                vec.tensor_tensor(out=lrow1[rows, :], in0=lrow1[rows, :], in1=q[rows, :], op=ALU.mult)\
                   .then_inc(q_ready, 1)
                dve.wait_ge(q_ready, p + 1)

            def read_cols(p):
                dve.wait_ge(cols_done, p + 1)
                vec.tensor_copy(q_col[:, bass.ds(p * B, B)], sm[:, 0:B]).then_inc(cols_read, 1)
                vec.tensor_scalar(out=no_edge[:, bass.ds(p * B, B)], in0=sm[:, B:2 * B], scalar1=0.0, scalar2=None,
                                  op0=ALU.is_le).then_inc(cols_read, 1)

            def evacuate1(p, par):
                link = Links(dve, evac1_links, 2, p)
                dve.wait_ge(main1, p * GROUPS + GROUPS)
                dve.wait_ge(xT_in, 16 * (p + 1))
                link(vec.scalar_tensor_tensor(out=xs[:, :], in0=ysum[:, :], scalar=0.0, in1=xT[:, :],
                                              op0=ALU.is_le, op1=ALU.mult))
                link(vec.tensor_tensor(out=xs[:, :], in0=xp[:, par, :], in1=xs[:, :], op=ALU.add))
                vec.tensor_tensor(out=xs[:, :], in0=xs[:, :], in1=q[:, :], op=ALU.mult).then_inc(evac1, 1)
                dve.wait_ge(evac1, p + 1)

            def row_stats(link, rows, blocks, into, done):
                for b in blocks:
                    last = vec.bn_stats(bns[:, b, :], rows(b))
                link(last)
                carry_wait()
                for b in blocks:
                    last = vec.bn_aggr(into[:, b, :], bns[:, b, :])
                last.then_inc(done, 1)

            def normalize1(p, j):
                dve.wait_ge(rstd1, p * 2 + j + 1)
                for b in (2 * j, 2 * j + 1):
                    last = vec.tensor_scalar(out=zn[:, b % 2, :], in0=z_of(b), scalar1=mv[:, b, 0:1],
                                             scalar2=rstd[:, b:b + 1], op0=ALU.subtract, op1=ALU.mult)
                last.then_inc(zn_ready, 1)

            def keep_tc(p, j):
                dve.wait_ge(tc_psum, p * 2 + j + 1)
                vec.tensor_tensor(out=tc[:, bass.ds(p * B + 2 * j, 2), :],
                                  in0=big[:, 3, :].rearrange("p (b d) -> p b d", b=2),
                                  in1=bias2[:, :].unsqueeze(1).to_broadcast([128, 2, 2 * D]), op=ALU.add)\
                   .then_inc(tc_ready, 1)

            def norm1(p):
                link = Links(dve, ln1_links, 2, p)
                for j in range(2):
                    dve.wait_ge(z_done, p * 2 + j + 1)
                    row_stats(link, z_of, (2 * j, 2 * j + 1), mv, ln1_stats)
                normalize1(p, 0)

            def second_half1(p):
                dve.wait_ge(hT_done, p * 2 + 1)
                normalize1(p, 1)
                keep_tc(p, 0)

            def layer1_step(p, par, loads, post, check, ahead):
                if post:
                    evacuate1(p - 1, 1 - par)
                stats(p, par)
                if check:
                    for g in (2, 3):
                        group_sum(p + 1, 1 - par, g, loads[1])
                if post:
                    norm1(p - 1)
                invert(p, par)
                if check:
                    thresholds(p + 1)
                if ahead:
                    group_sum(p + 2, par, 0, loads[2])
                if check:
                    compare(p + 1, 1 - par)
                if post:
                    second_half1(p - 1)
                read_cols(p)
                if check:
                    mask(p + 1, 1 - par)
                if ahead:
                    group_sum(p + 2, par, 1, loads[2])
                if post:
                    keep_tc(p - 1, 1)

            for g in range(GROUPS):
                group_sum(0, 0, g, 1)
            setup()
            thresholds(0)
            compare(0, 0)
            mask(0, 0)
            for g in (0, 1):
                group_sum(1, 1, g, 1)
            layer1_panels(dve, layer1_step)

            def self_loops(p):
                for b in range(B):
                    last = vec.tensor_scalar(out=loop_d[:, b, :], in0=ident[:, :],
                                             scalar1=no_edge[:, bass.ds(p * B + b, 1)], scalar2=None, op0=ALU.mult)
                last.then_inc(loops_ready, 1)

            def spread(row):
                return row[:, :].unsqueeze(1).to_broadcast([128, B, D])

            def finish2(p, piece):
                here = bass.ds(p * B, B)
                link = Links(dve, ln2_links, 7, p, before=(0, 1, 2, 3, 5, 7, 7, 7)[piece])
                if piece == 0:
                    dve.wait_ge(z2_done, p + 1)
                    for b in range(B):
                        last = vec.scalar_tensor_tensor(out=r[:, b, :], in0=st4[:, b, :],
                                                        scalar=q_col[:, bass.ds(p * B + b, 1)],
                                                        in1=tc[:, bass.ds(p * B + b, 1), D:2 * D]
                                                        .rearrange("p a d -> p (a d)"),
                                                        op0=ALU.mult, op1=ALU.add)
                    link(last)
                if piece == 1:
                    row_stats(link, lambda b: r[:, b, :], range(B), mv2, ln2_stats)
                if piece == 2:
                    dve.wait_ge(rstd2_ready, p * 3 + 1)
                    for b in range(B):
                        last = vec.tensor_scalar(out=r[:, b, :], in0=r[:, b, :], scalar1=mv2[:, b, 0:1],
                                                 scalar2=rstd2[:, 0, b:b + 1], op0=ALU.subtract, op1=ALU.mult)
                    link(last)
                if piece == 3:
                    link(vec.tensor_tensor(out=r[:, :, :], in0=r[:, :, :], in1=spread(gamma2), op=ALU.mult))
                    link(vec.tensor_tensor(out=r[:, :, :], in0=r[:, :, :], in1=spread(beta2), op=ALU.add))
                if piece == 4:
                    link(vec.scalar_tensor_tensor(out=r[:, :, :], in0=r[:, :, :], scalar=0.0, in1=x[:, here, :],
                                                  op0=ALU.max, op1=ALU.add))
                    row_stats(link, lambda b: r[:, b, :], range(B), mv2, ln2_stats)
                if piece == 5:
                    dve.wait_ge(rstd2_ready, p * 3 + 3)
                    for b in range(B):
                        last = vec.tensor_scalar(out=r2[:, b, :], in0=r[:, b, :], scalar1=mv2[:, b, 0:1],
                                                 scalar2=rstd2[:, 1, b:b + 1], op0=ALU.subtract, op1=ALU.mult)
                    last.then_inc(u_ready, 1)
                if piece == 6:
                    for b in range(B):
                        last = vec.tensor_scalar(out=x[:, bass.ds(p * B + b, 1), :].rearrange("p a d -> p (a d)"),
                                                 in0=r[:, b, :], scalar1=mv2[:, b, 0:1],
                                                 scalar2=rstd2[:, 0, b:b + 1], op0=ALU.subtract, op1=ALU.mult)
                    last.then_inc(x_ready, 1)
                if piece == 7:
                    dve.wait_ge(x_ready, p + 1)
                    dve.wait_ge(uTh_ready, p + 1)
                    cols = bass.ds(p * W, W)
                    vec.tensor_tensor(out=uTl[:, cols], in0=sm[:, :], in1=uTh[:, cols].bitcast(F32),
                                      op=ALU.subtract).then_inc(uTl_ready, 1)

            evacuate1(P - 1, 1)
            norm1(P - 1)
            second_half1(P - 1)
            keep_tc(P - 1, 1)
            dve.wait_ge(cols_read, 2 * P)
            self_loops(0)
            dve.wait_ge(consts2_in, 16 * len(CONSTS2))
            dve.wait_ge(tc_ready, 2 * P)
            messages = tc[:, :, 0:D].rearrange("p (n two) d -> p n two d", two=2)
            for g in range(GROUPS):
                own = slice(g * SG, (g + 1) * SG)
                vec.tensor_copy(th[:, own, :], messages[:, own, 1, :]).then_inc(th_ready, 1)
                dve.wait_ge(th_ready, g + 1)
                vec.tensor_tensor(out=tl[:, own, :], in0=messages[:, own, 1, :], in1=th[:, own, :].bitcast(F32),
                                  op=ALU.subtract).then_inc(tl_ready, 1)

            def adj_low(p, n):
                dve.wait_ge(ah_ready, (p - 1) * S2 + n + 1)
                vec.tensor_tensor(out=al[:, n % RING2, :], in0=adjA[:, SPLIT2[n], :],
                                  in1=ah[:, n % RING2, :].bitcast(F32), op=ALU.subtract).then_inc(al_ready, 1)

            def layer2_step(p, par):
                for n in range(S2):
                    adj_low(p, n)
                    if n == LOOPS_AFTER:
                        dve.wait_ge(main2, p * GROUPS)
                        self_loops(p)
                    if n in FINISH2_AFTER:
                        finish2(p - 1, FINISH2_AFTER.index(n))

            panels(dve, layer2_step)
            layer2_step(P - 1, 1)

            def finish3(p, piece):
                here = bass.ds(p * B, B)
                link = Links(dve, ln3_links, 4, p, before=(0, 2, 3, 4)[piece])
                if piece == 0:
                    link(vec.tensor_tensor(out=r[:, :, :], in0=x[:, here, :], in1=spread(bias3), op=ALU.add))
                    dve.wait_ge(z3_done, p + 1)
                    link(vec.reciprocal(rden[:, :], sm[:, 0:B]))
                if piece == 1:
                    for b in range(B):
                        last = vec.scalar_tensor_tensor(out=r[:, b, :], in0=st4[:, b, :], scalar=rden[:, b:b + 1],
                                                        in1=r[:, b, :], op0=ALU.mult, op1=ALU.add)
                    link(last)
                if piece == 2:
                    row_stats(link, lambda b: r[:, b, :], range(B), mv2, ln3_stats)
                if piece == 3:
                    dve.wait_ge(rstd3, p + 1)
                    if not (isinstance(p, int) and p == 0):
                        dve.wait_ge(out_stored, 16 * p)
                    for b in range(B):
                        last = vec.tensor_scalar(out=r2[:, b, :], in0=r[:, b, :], scalar1=mv2[:, b, 0:1],
                                                 scalar2=rstd2[:, 0, b:b + 1], op0=ALU.subtract, op1=ALU.mult)
                    last.then_inc(out_ready, 1)
                    dve.wait_ge(out_ready, p + 1)

            def split_x(g):
                rows = x[:, 2 * g:2 * g + 2, 0:D - 1]
                if g in WHOLE:
                    n = WHOLE.index(g)
                    vec.tensor_copy(xo[:, 2 * n:2 * n + 2, 0:D - 1], rows).then_inc(xo_ready, 1)
                    return
                n = SPLIT.index(g)
                high = xh[:, 2 * n:2 * n + 2, 0:D - 1]
                vec.tensor_copy(high, rows).then_inc(xh_ready, 1)
                dve.wait_ge(xh_ready, n + 1)
                vec.tensor_tensor(out=xl[:, 2 * n:2 * n + 2, 0:D - 1], in0=rows, in1=high.bitcast(F32),
                                  op=ALU.subtract).then_inc(xl_ready, 1)

            def weights(p, g, first):
                if g in WHOLE:
                    n = WHOLE.index(g)
                    if not (first and n == 0):
                        dve.wait_ge(pv_done, (p if n else p - 1) * PAIRS + WHOLE[n - 1] + 1)
                    into = pn[:, :]
                else:
                    n = SPLIT.index(g)
                    if not (first and n < 2):
                        dve.wait_ge(pl_ready, p * S + n - 1)
                    into = pw[:, n % 2, :]
                vec.tensor_tensor(out=into, in0=e[:, g % 2, :],
                                  in1=adjA[:, 2 * g:2 * g + 2, :].rearrange("p a w -> p (a w)"), op=ALU.mult)\
                   .then_inc(w_ready, 1)

            def weights_low(p, g):
                n = SPLIT.index(g)
                high, low = ph[:, n % 4, :], pl[:, n % 4, :]
                if g in HIGH_ON_DVE:
                    if not (isinstance(p, int) and p == 0 and n < 4):
                        dve.wait_ge(pv_done, products_done(p, n - 4))
                    dve.wait_ge(w_ready, p * PAIRS + g + 1)
                    vec.tensor_copy(high, pw[:, n % 2, :]).then_inc(ph_dve, 1)
                    dve.wait_ge(ph_dve, p * len(HIGH_ON_DVE) + HIGH_ON_DVE.index(g) + 1)
                else:
                    dve.wait_ge(ph_ready, p * len(HIGH_ON_ACT) + HIGH_ON_ACT.index(g) + 1)
                vec.tensor_tensor(out=low, in0=pw[:, n % 2, :], in1=high.bitcast(F32), op=ALU.subtract)\
                   .then_inc(pl_ready, 1)

            def layer3_step(p, par, post, first=False):
                for g in range(PAIRS):
                    if FINISH_AT <= g < FINISH_AT + 4 and post is not None:
                        finish3(post, g - FINISH_AT)
                    if first:
                        if 1 <= g < 8:
                            finish2(P - 1, g - 1)
                        if g == LAST_U_AT + 2:
                            finish2(P - 1, 7)
                        split_x(g)
                    slot = g // (TG // 2)
                    if g % (TG // 2) == 0:
                        dve.wait_ge(slot_in[0][slot], (p + (P // 2 + P + 1)) * 16)
                    dve.wait_ge(exp_done, p * PAIRS + g + 1)
                    weights(p, g, first)
                    if g - 1 in SPLIT:
                        weights_low(p, g - 1)

            vec.tensor_tensor(out=w3[:, :], in0=w3[:, :], in1=w3_last[:, :], op=ALU.subtract).then_inc(w3_ready, 1)
            dve.wait_ge(main2, P * GROUPS)
            vec.tensor_copy(xh[:, :, D - 1], ones[:, 0:2 * S]).then_inc(x_last_ready, 1)
            vec.tensor_copy(xo[:, :, D - 1], ones[:, 0:2 * len(WHOLE)]).then_inc(x_last_ready, 1)
            vec.tensor_scalar(out=xl[:, :, D - 1], in0=ones[:, 0:2 * S], scalar1=0.0, scalar2=None, op0=ALU.mult)\
               .then_inc(x_last_ready, 1)
            layer3_step(0, 0, None, first=True)
            layer3_step(1, 1, 0)
            with dve.Fori(0, LOOPS) as i:
                layer3_step(i * 2 + 2, 0, i * 2 + 1)
                layer3_step(i * 2 + 3, 1, i * 2 + 2)
            for piece in range(4):
                finish3(P - 1, piece)

        @block.tensor
        def _(pe):
            mm = nc.tensor.matmul
            pe.wait_ge(pool_consts, 6)
            pe.wait_ge(consts_in, 16 * N_CONSTS)
            for h in range(2):
                mm(big[:, 0, 0:H], w_in1T[:, h, :], w_out1[:, h, :], start=h == 0, stop=h == 1)
            for h in range(2):
                last = mm(big[0:1, 1, 0:H], b_in1[:, h:h + 1], w_out1[:, h, :], start=h == 0, stop=h == 1)
            last.then_inc(setup_mm, 1)

            def column_sums(p, par):
                pe.wait_ge(sums_links, (2 * GROUPS - 1) * (p + 1))
                mm(st[:, :], ones[:, :], sums[:, par, :], start=True, stop=True).then_inc(csum_done, 1)

            def count(p):
                pe.wait_ge(diff_ready, p + 1)
                mm(sm[0:1, 8:9], cdiff[:, :], ones[:, 0:1], start=True, stop=True).then_inc(count_done, 1)

            def z_products(p, par):
                rows = slice(32 * par, 32 * par + 3)
                pe.wait_ge(evac1, p + 1)
                for b in range(B):
                    cols = slice(b * 128, (b + 1) * 128)
                    mm(z_of(b), xs[:, cols], v1[:, :], start=True, stop=False)
                    mm(z_of(b), xT[:, cols], w_self1[:, :], start=False, stop=False)
                    last = mm(z_of(b), lrow1[rows, cols], brow1[rows, :], start=False, stop=True)
                    if b % 2:
                        last.then_inc(z_done, 1)

            def transposes(p, j):
                pe.wait_ge(zn_ready, p * 2 + j + 1)
                for b in range(2):
                    for h in range(2):
                        last = nc.tensor.transpose(big[:, 2, h * 256 + b * 128:h * 256 + (b + 1) * 128],
                                                   zn[:, b, h * 128:(h + 1) * 128], ident[:, :])
                last.then_inc(hT_done, 1)

            def tc_products(p, j):
                pe.wait_ge(h1T_ready, p * 2 + j + 1)
                if j:
                    pe.wait_ge(tc_ready, p * 2 + 1)
                for b in range(2):
                    for h in range(2):
                        last = mm(big[:, 3, b * 256:(b + 1) * 256], h1T[:, h, b, :], w_cat2[:, h, :],
                                  start=h == 0, stop=h == 1)
                last.then_inc(tc_psum, 1)

            def columns(p):
                pe.wait_ge(q_ready, p + 1)
                for i, row in enumerate((q, ysum)):
                    for b in range(B):
                        last = mm(sm[:, i * B + b:i * B + b + 1], row[0:1, b * 128:(b + 1) * 128], ones[0:1, 0:1],
                                  start=True, stop=True)
                last.then_inc(cols_done, 1)

            def main(par, src, lhs, g, done, part=slice(0, TG)):
                for k in range(g * TG, (g + 1) * TG)[part]:
                    last = mm(xp[:, par, :], lhs(k), src[:, k, :], start=k == 0, stop=k == TILES - 1)
                if part.stop == TG:
                    last.then_inc(done, 1)

            def layer1_step(p, par, loads, post, check, ahead):
                def main1_group(g, part=slice(0, TG)):
                    main(par, adj_of[par], lambda k: x[:, k, :], g, main1, part)

                pe.wait_ge(panel_ready, p + 1)
                mm(st[:, :], ones[:, :], sums[:, par, :], start=True, stop=True).then_inc(ysum_done, 1)
                main1_group(0)
                if post:
                    z_products(p - 1, 1 - par)
                main1_group(1)
                if check:
                    pe.wait_ge(ysum_read, p + 1)
                    column_sums(p + 1, 1 - par)
                if post:
                    transposes(p - 1, 0)
                main1_group(2)
                if post:
                    tc_products(p - 1, 0)
                columns(p)
                main1_group(3, slice(0, TG // 2))
                if post:
                    transposes(p - 1, 1)
                if check:
                    pe.wait_ge(cols_read, 2 * p + 2)
                    count(p + 1)
                main1_group(3, slice(TG // 2, TG))
                if post:
                    tc_products(p - 1, 1)
                else:
                    pe.wait_ge(brow_copied, 16)

            column_sums(0, 0)
            count(0)
            pe.wait_ge(x_in, 16)
            layer1_panels(pe, layer1_step)

            def main2_group(p, par, g):
                pe.wait_ge(group_masked, p * GROUPS + g + 1)
                if g == GROUPS - 1:
                    pe.wait_ge(t2s_ready, p + 1)
                    pe.wait_ge(loops_ready, p + 1)
                    for b in range(B):
                        mm(xp[:, par, b * 128:(b + 1) * 128], t2s[:, b, :], loop_d[:, b, :], start=False, stop=False)
                main(par, adjA, lambda k: tc[:, k, 0:D], g, main2)

            def split2_group(p, par, g, between):
                pe.wait_ge(group_masked, p * GROUPS + g + 1)
                if g == GROUPS - 1:
                    pe.wait_ge(t2s_ready, p + 1)
                    pe.wait_ge(loops_ready, p + 1)
                    for b in range(B):
                        mm(xp[:, par, b * 128:(b + 1) * 128], t2s[:, b, :], loop_d[:, b, :], start=False, stop=False)
                for k in range(g * TG, (g + 1) * TG):
                    if k not in SPLIT2:
                        mm(xp[:, par, :], tc[:, k, 0:D], adjA[:, k, :], start=k == 0, stop=False)
                    else:
                        n = SPLIT2.index(k)
                        high, low = ah[:, n % RING2, :], al[:, n % RING2, :]
                        pe.wait_ge(al_ready, (p - 1) * S2 + n + 1)
                        mm(xp[:, par, :], th[:, n, :], high, start=False, stop=False)
                        mm(xp[:, par, :], tl[:, n, :], high, start=False, stop=False)
                        mm(xp[:, par, :], th[:, n, :], low, start=False, stop=n == S2 - 1)\
                            .then_inc(split_used(p, n)[0], 1)
                    if k == g * TG:
                        between()

            def z2_products(p):
                pe.wait_ge(evac2, p + 1)
                for b in range(B):
                    last = mm(st4[:, b, :], xs2[:, b * 128:(b + 1) * 128], w_out2[:, :], start=True, stop=True)
                last.then_inc(z2_done, 1)

            def u_transposes(p):
                pe.wait_ge(u_ready, p + 1)
                for b in range(B):
                    last = nc.tensor.transpose(sm[:, b * 128:(b + 1) * 128], r2[:, b, :], ident[:, :])
                last.then_inc(uT_done, 1)

            def rows_known(g):
                pe.wait_ge(tc_ready, 2 * (((g + 1) * TG + B - 1) // B))

            rows_known(0)
            main2_group(0, 0, 0)
            z_products(P - 1, 1)
            rows_known(1)
            main2_group(0, 0, 1)
            transposes(P - 1, 0)
            rows_known(2)
            main2_group(0, 0, 2)
            tc_products(P - 1, 0)
            transposes(P - 1, 1)
            tc_products(P - 1, 1)
            rows_known(3)
            main2_group(0, 0, 3)
            pe.wait_ge(consts2_in, 16 * len(CONSTS2))

            pe.wait_ge(tl_ready, GROUPS)

            def layer2_step(p, par):
                split2_group(p, par, 0, between=lambda: z2_products(p - 1))
                for g in range(1, GROUPS - 1):
                    split2_group(p, par, g, between=lambda: None)
                split2_group(p, par, GROUPS - 1, between=lambda: u_transposes(p - 1))

            panels(pe, layer2_step)
            layer2_step(P - 1, 1)

            def scores(p, g, first):
                if first:
                    pe.wait_ge(uTl_ready, (2 * g + 1) // B + 1)
                if not (first and g < 2):
                    pe.wait_ge(exp_done, p * PAIRS + g - 1)
                cols = bass.ds(p * W, W)
                for k in range(2):
                    tile = slice((2 * g + k) * 128, (2 * g + k + 1) * 128)
                    s = big[:, 2 * (g % 2) + k, :]
                    mm(s, uTh[:, tile], uTh[:, cols], start=True, stop=False)
                    mm(s, uTh[:, tile], uTl[:, cols], start=False, stop=False)
                    last = mm(s, uTl[:, tile], uTh[:, cols], start=False, stop=True)
                last.then_inc(s_done, 1)

            def weighted(p, par, g, first=False):
                if g in WHOLE:
                    n = WHOLE.index(g)
                    pe.wait_ge(w_ready, p * PAIRS + g + 1)
                    if first:
                        pe.wait_ge(xo_ready, n + 1)
                    terms = ((xo, pn[:, :]),)
                else:
                    n = SPLIT.index(g)
                    pe.wait_ge(pl_ready, p * S + n + 1)
                    if first:
                        pe.wait_ge(xl_ready, n + 1)
                    high, low = ph[:, n % 4, :], pl[:, n % 4, :]
                    terms = ((xh, high), (xl, high), (xh, low))
                for k in range(2):
                    for rows, w in terms:
                        last = mm(xp[:, par, :], rows[:, 2 * n + k, :], w[:, k * W:(k + 1) * W],
                                  start=g == 0 and k == 0 and rows is xh and w is high,
                                  stop=g == PAIRS - 1 and k == 1)
                last.then_inc(pv_done, 1)

            def z3_products(p, par):
                pe.wait_ge(evac3, p + 1)
                for b in range(B):
                    cols = slice(b * 128, (b + 1) * 128)
                    mm(st4[:, b, :], xs2[:, cols], w3[:, :], start=True, stop=True)
                    last = mm(sm[:, b:b + 1], xs2[:, cols], ident[:, D - 1:D], start=True, stop=True)
                last.then_inc(z3_done, 1)

            def layer3_step(p, par, first=False):
                for g in range(PAIRS):
                    if first and g == 1:
                        z2_products(P - 1)
                    if first and g == LAST_U_AT:
                        u_transposes(P - 1)
                    scores(p, g, first)
                    if g >= LAG:
                        weighted(p, par, g - LAG, first)
                    elif not first:
                        weighted(p - 1, 1 - par, PAIRS - LAG + g)
                    if g == Z3_AT and not first:
                        z3_products(p - 1, 1 - par)

            layer3_step(0, 0, first=True)
            pe.wait_ge(w3_ready, 1)
            panels(pe, layer3_step)
            layer3_step(P - 1, 1)
            for g in range(PAIRS - LAG, PAIRS):
                weighted(P - 1, 1, g)
            z3_products(P - 1, 1)


LOOPS_AFTER = 7
FINISH2_AFTER = (1, 2, 4, 5, 8, 10, 12, 15)

LAST_U_AT = 8

Z3_AT = 6
FINISH_AT = 7
LAG = 3
WHOLE_EVERY = 4
HIGH_ON_DVE = (4, 12)


def layouts(i):
    import numpy as np

    def blocks(a):
        return a.reshape(-1, 128, a.shape[1]).transpose(1, 0, 2)

    def panels_of(a):
        n = a.shape[0]
        return a.reshape(n // 128, 128, n // W, W).transpose(2, 1, 0, 3)

    def over_partitions(a):
        return np.broadcast_to(a.reshape(1, -1), (128, a.size))

    x, adj = i["x"], i["adj"]
    n = x.shape[0]
    out = {
        "x": blocks(x),
        "xT": x.T.reshape(x.shape[1], n // W, W).transpose(1, 0, 2),
        "adj": panels_of(adj),
        "adjT": panels_of(adj.T),
        "w_in1T": blocks(i["L0_gnn_W_in1"].T),
        "w_out1": blocks(i["L0_gnn_W_out1"]),
        "w_self1": i["L0_gnn_W_self1"],
        "b_in1": i["L0_gnn_b_in1"].reshape(2, 128).T,
        "b_out1": i["L0_gnn_b_out1"].reshape(1, -1),
        "b_self1": i["L0_gnn_b_self1"].reshape(1, -1),
        "g1": i["L0_gnn_g1"].reshape(2, 128).T,
        "be1": i["L0_gnn_be1"].reshape(2, 128).T,
        "w_cat2": blocks(np.concatenate([i["L0_gnn_W_in2"], i["L0_gnn_W_self2"]], axis=1)),
        "b_in2": over_partitions(i["L0_gnn_b_in2"]),
        "b_out2": over_partitions(i["L0_gnn_b_out2"]),
        "b_self2": over_partitions(i["L0_gnn_b_self2"]),
        "w_out2": i["L0_gnn_W_out2"],
        "g2": over_partitions(i["L0_gnn_g2"]),
        "be2": over_partitions(i["L0_gnn_be2"]),
        "w3T": i["L1_gnn_W"].T,
        "w3T_last": over_partitions(i["L1_gnn_W"][:, -1]),
        "bias3": over_partitions(i["L1_gnn_bias"]),
        "b": over_partitions(i["L1_gnn_b"]),
    }
    return {k: np.ascontiguousarray(v) for k, v in out.items()}


def kernel(**inputs):
    import numpy as np
    import concourse.bacc as bacc
    from concourse.bass_utils import run_bass_kernel_spmd

    arrays = layouts({k: np.asarray(v) for k, v in inputs.items()})
    n, d = np.asarray(inputs["x"]).shape
    nc = bacc.Bacc("TRN2", target_bir_lowering=False, num_devices=1)
    tensors = {k: nc.dram_tensor(f"in_{k}", a.shape, mybir.dt.from_np(a.dtype), kind="ExternalInput").ap()
               for k, a in arrays.items()}
    tensors["out"] = nc.dram_tensor("out_rows", (n // W, 128, B, d), F32, kind="ExternalOutput").ap()
    build_program(nc, tensors)
    result = run_bass_kernel_spmd(nc, [{f"in_{k}": a for k, a in arrays.items()}], core_ids=[0])
    rows = result.results[0]["out_rows"]
    return rows.transpose(0, 2, 1, 3).reshape(n, d)
```
